# Optimizing a Trainium2 kernel written in Bass

```python
import numpy as np
import jax
import jax.numpy as jnp

def _softmax(x, axis=-1):
    return jax.nn.softmax(x, axis=axis)

def _gelu(x):
    return jax.nn.gelu(x, approximate=True)

def _silu(x):
    return jax.nn.silu(x)

def _sigmoid(x):
    return jax.nn.sigmoid(x)

def _layernorm(x, axis=-1, eps=1e-05):
    m = jnp.mean(x, axis=axis, keepdims=True)
    v = jnp.var(x, axis=axis, keepdims=True)
    return (x - m) / jnp.sqrt(v + eps)

def _scatter_add(tgt, idx, src, axis=0):
    return tgt.at[idx].add(src)

def _segment_sum(src, seg, n):
    return jax.ops.segment_sum(src, seg, n)
kernel_name = 'mk_seq_postln_d1_jaxref_r8_83b021'

def setup_inputs(seed: int=0):
    np.random.seed(seed)
    _w = jnp.asarray

    def _L0_attn_setup():
        import jax, jax.numpy as jnp
        import numpy as np
        B, S, D = (4, 256, 128)

        def _xavier(key, shape):
            bound = float(np.sqrt(6.0 / (shape[0] + shape[1])))
            return jax.random.uniform(key, shape, dtype=jnp.float32, minval=-bound, maxval=bound)
        key = jax.random.key(seed)
        k0, k1, k2, k3 = jax.random.split(key, 4)
        return {'embeddings': jax.random.normal(k0, (B, S, D), dtype=jnp.float32), 'W_Q': _xavier(k1, (D, D)), 'W_K': _xavier(k2, (D, D)), 'W_V': _xavier(k3, (D, D))}
    _L0_attn_in = _L0_attn_setup()

    def _L0_ffn_setup():
        import jax, jax.numpy as jnp
        import numpy as np
        TOP_K = 2
        TEMP = 0.9
        EPS = 1e-05
        B, S, D, F, E = (2, 256, 128, 512, 8)

        def _moe_forward(x, gate_w, gate_b, w1, b1, w2, b2, ln_g, ln_b):
            logits = (x @ gate_w + gate_b) / TEMP
            topk_vals, topk_idx = jax.lax.top_k(logits, TOP_K)
            keep = jax.nn.one_hot(topk_idx, E, dtype=jnp.bool_).any(-2)
            masked = jnp.where(keep, logits, -jnp.inf)
            gate_probs = jax.nn.softmax(masked, axis=-1)
            h = jnp.einsum('bsd,edf->bsef', x, w1) + b1
            h = jax.nn.gelu(h, approximate=False)
            expert_out = jnp.einsum('bsef,efd->bsed', h, w2) + b2
            out = jnp.einsum('bse,bsed->bsd', gate_probs, expert_out)
            mu = out.mean(-1, keepdims=True)
            var = out.var(-1, keepdims=True)
            out = (out - mu) / jnp.sqrt(var + EPS) * ln_g + ln_b
            return out
        key = jax.random.key(seed)
        ks = jax.random.split(key, 4)
        scale_in = 1.0 / np.sqrt(D)
        scale_ff = 1.0 / np.sqrt(F)
        return {'x': jax.random.normal(ks[0], (B, S, D), jnp.float32), 'gate_w': jax.random.normal(ks[1], (D, E), jnp.float32) * scale_in, 'gate_b': jnp.zeros((E,), jnp.float32), 'w1': jax.random.normal(ks[2], (E, D, F), jnp.float32) * scale_in, 'b1': jnp.zeros((E, F), jnp.float32), 'w2': jax.random.normal(ks[3], (E, F, D), jnp.float32) * scale_ff, 'b2': jnp.zeros((E, D), jnp.float32), 'ln_g': jnp.ones((D,), jnp.float32), 'ln_b': jnp.zeros((D,), jnp.float32)}
    _L0_ffn_in = _L0_ffn_setup()
    _d = {'L0_attn_embeddings': _L0_attn_in['embeddings'], 'L0_attn_W_Q': _L0_attn_in['W_Q'], 'L0_attn_W_K': _L0_attn_in['W_K'], 'L0_attn_W_V': _L0_attn_in['W_V'], 'L0_ffn_gate_w': _L0_ffn_in['gate_w'], 'L0_ffn_gate_b': _L0_ffn_in['gate_b'], 'L0_ffn_w1': _L0_ffn_in['w1'], 'L0_ffn_b1': _L0_ffn_in['b1'], 'L0_ffn_w2': _L0_ffn_in['w2'], 'L0_ffn_b2': _L0_ffn_in['b2'], 'L0_ffn_ln_g': _L0_ffn_in['ln_g'], 'L0_ffn_ln_b': _L0_ffn_in['ln_b']}
    _x0 = _d['L0_attn_embeddings']
    _d['L0_attn_embeddings'] = jax.random.normal(jax.random.fold_in(jax.random.key(seed), 1), (8, 512, 128), dtype=_x0.dtype)
    del _x0
    return _d

def reference(L0_attn_embeddings, L0_attn_W_Q, L0_attn_W_K, L0_attn_W_V, L0_ffn_gate_w, L0_ffn_gate_b, L0_ffn_w1, L0_ffn_b1, L0_ffn_w2, L0_ffn_b2, L0_ffn_ln_g, L0_ffn_ln_b):

    def _L0_attn_ref(embeddings, W_Q, W_K, W_V):
        import jax, jax.numpy as jnp
        import numpy as np
        B, S, D = (4, 256, 128)

        def _xavier(key, shape):
            bound = float(np.sqrt(6.0 / (shape[0] + shape[1])))
            return jax.random.uniform(key, shape, dtype=jnp.float32, minval=-bound, maxval=bound)
        _, seq_len, d = embeddings.shape
        Q = embeddings @ W_Q
        K = embeddings @ W_K
        V = embeddings @ W_V
        scale = 1.0 / jnp.sqrt(jnp.float32(d))
        scores = jnp.einsum('bqd,bkd->bqk', Q, K) * scale
        causal = jnp.tril(jnp.ones((seq_len, seq_len), dtype=bool))
        scores = jnp.where(causal[None, :, :], scores, -jnp.inf)
        probs = jax.nn.softmax(scores, axis=-1)
        return jnp.einsum('bqk,bkd->bqd', probs, V)

    def _L0_ffn_ref(x, gate_w, gate_b, w1, b1, w2, b2, ln_g, ln_b):
        import jax, jax.numpy as jnp
        import numpy as np
        TOP_K = 2
        TEMP = 0.9
        EPS = 1e-05
        B, S, D, F, E = (2, 256, 128, 512, 8)

        def _moe_forward(x, gate_w, gate_b, w1, b1, w2, b2, ln_g, ln_b):
            logits = (x @ gate_w + gate_b) / TEMP
            topk_vals, topk_idx = jax.lax.top_k(logits, TOP_K)
            keep = jax.nn.one_hot(topk_idx, E, dtype=jnp.bool_).any(-2)
            masked = jnp.where(keep, logits, -jnp.inf)
            gate_probs = jax.nn.softmax(masked, axis=-1)
            h = jnp.einsum('bsd,edf->bsef', x, w1) + b1
            h = jax.nn.gelu(h, approximate=False)
            expert_out = jnp.einsum('bsef,efd->bsed', h, w2) + b2
            out = jnp.einsum('bse,bsed->bsd', gate_probs, expert_out)
            mu = out.mean(-1, keepdims=True)
            var = out.var(-1, keepdims=True)
            out = (out - mu) / jnp.sqrt(var + EPS) * ln_g + ln_b
            return out
        return _moe_forward(x, gate_w, gate_b, w1, b1, w2, b2, ln_g, ln_b)
    x = L0_attn_embeddings
    x = _layernorm(x + _L0_attn_ref(x, L0_attn_W_Q, L0_attn_W_K, L0_attn_W_V), axis=-1)
    x = _layernorm(x + _L0_ffn_ref(x, L0_ffn_gate_w, L0_ffn_gate_b, L0_ffn_w1, L0_ffn_b1, L0_ffn_w2, L0_ffn_b2, L0_ffn_ln_g, L0_ffn_ln_b), axis=-1)
    return x

_drawn_inputs = setup_inputs


def setup_inputs(seed=0):
    import zlib

    import numpy as np

    out = dict(_drawn_inputs(seed))
    spreads = {'L0_ffn_gate_b': (0.0, 0.1),
     'L0_ffn_b1': (0.0, 0.1),
     'L0_ffn_b2': (0.0, 0.1),
     'L0_ffn_ln_g': (1.0, 0.2),
     'L0_ffn_ln_b': (0.0, 0.1)}
    factors = {}
    for name, (base, spread) in spreads.items():
        noise = np.random.default_rng([zlib.crc32(name.encode()), seed]).standard_normal(out[name].shape)
        drawn = base * np.exp(spread * noise) if base else spread * noise
        out[name] = jnp.asarray(drawn.astype(out[name].dtype))
    for name, factor in factors.items():
        out[name] = (out[name] * factor).astype(out[name].dtype)
    return out
```

```python
from contextlib import ExitStack

import concourse.bass as bass
from concourse import mybir

F32 = mybir.dt.float32
F16 = mybir.dt.float16
BF16 = mybir.dt.bfloat16
I32 = mybir.dt.int32
U32 = mybir.dt.uint32
ALU = mybir.AluOpType
ACT = mybir.ActivationFunctionType
AX = mybir.AxisListType

P = 128
GROUPS = (3, 5)
UNROLL = 4
LAG = 2
TEMPERATURE = 0.9
EPS = 1e-5
WSCALE = 64.0
MASKED = -1e30
RSQRT_MAGIC = float(0x5F3759DF)
NEWTON = 3


def moe_block(nc, emb, W_Q, W_K, W_V, gate_w, gate_b, w1, b1, w2, b2, ln_g, ln_b, out):
    B, S, D = emb.shape
    E, _, F = w1.shape
    TB = S // P
    NT = B * TB
    N = NT * P
    FC = F // P
    TOPK = 2
    SCALE = float(D) ** -0.5
    assert D == P and TB == 4 and sum(GROUPS) == B and E == 8

    group_tiles, group_first, group_b0 = [], [], []
    for g, nb in enumerate(GROUPS):
        need = nb * TB * TOPK + E - 1
        group_first.append(sum(group_tiles))
        group_b0.append(sum(GROUPS[:g]))
        group_tiles.append((need + UNROLL - 1) // UNROLL * UNROLL)
    J = sum(group_tiles)
    PREFILL = J // B
    assert J % B == 0
    ROW = D + 2
    GATE, BACK = D, D + 1

    slots = nc.dram_tensor("slots", [J * P, ROW], F32, kind="Internal").ap()
    returned = nc.dram_tensor("returned", [TOPK * N + J * P, D], F32, kind="Internal").ap()

    ctx = ExitStack()
    with ctx:
        def sb(name, shape, dt=F32):
            return ctx.enter_context(nc.sbuf_tensor(name, shape, dt))

        def sem(name):
            return ctx.enter_context(nc.semaphore(name))

        ident = sb("ident", [P, P])
        ident_h = sb("ident_h", [P, P], F16)
        ident_b = sb("ident_b", [P, P], BF16)
        mask = sb("mask", [P, P], BF16)
        before = sb("before", [P, P], F16)
        ones_h = sb("ones_h", [P, P], F16)
        ones = sb("ones", [P, 64])
        expert_id = sb("expert_id", [P, E])
        tile_start = sb("tile_start", [1, max(group_tiles)])
        wq, wk, wv = (sb(n, [P, D]) for n in ("wq", "wk", "wv"))
        wqkT = sb("wqkT", [P, 2 * D])
        mqk = sb("mqk", [P, D])
        x_in = sb("x_in", [P, TB, D])
        x_res = sb("x_res", [P, TB, D])
        xT = sb("xT", [P, S])
        gT = sb("gT", [P, S])
        v = sb("v", [P, TB, D])
        OFF = [P * i * (i + 1) // 2 for i in range(TB + 1)]
        probs = sb("probs", [P, OFF[TB]])
        probsT = sb("probsT", [P, OFF[TB]])
        rowmax = sb("rowmax", [P, NT])
        negmax = sb("negmax", [P, NT])
        rowsum = sb("rowsum", [P, NT])
        rinv = sb("rinv", [P, TB])
        z = sb("z", [P, TB, D])
        stats = sb("stats", [P, TB, 6])
        moments = sb("moments", [P, TB, 2])
        rstd = sb("rstd", [P, TB])
        var, square = sb("var", [P, TB]), sb("square", [P, TB])
        xn = sb("xn", [P, TB, D])
        xnT = sb("xnT", [P, S])
        x_halves = sb("x_halves", [P, TB, 2 * D], F16)
        x1b = sb("x1b", [P, NT, D])
        gw = sb("gw", [P, E])
        gb = sb("gb", [P, E])
        lng = sb("lng", [P, D])
        lnb = sb("lnb", [P, D])
        logits = sb("logits", [P, TB, E])
        top = sb("top", [P, TB, E])
        topi = sb("topi", [P, TB, E], U32)
        topf = sb("topf", [P, TB, TOPK])
        gap = sb("gap", [P, NT])
        egap = sb("egap", [P, NT])
        p1 = sb("p1", [P, NT])
        chosen = sb("chosen", [P, TOPK, NT, E], F16)
        NG = max(GROUPS) * TB * TOPK
        total = sb("total", [P, NG, E])
        running = sb("running", [P, NG, E])
        place = sb("place", [P, NG, E])
        padded_i = sb("padded_i", [P, E], I32)
        padded = sb("padded", [P, E])
        ends = sb("ends", [P, E])
        base = sb("base", [P, E])
        slot_f = sb("slot_f", [P, NG])
        slot_of = sb("slot_of", [P, len(GROUPS), NG], U32)
        passed = sb("passed", [1, max(group_tiles), E])
        passed_n = sb("passed_n", [1, max(group_tiles)])
        expert_of = sb("expert_of", [1, LAG + J + 2], I32)
        rows = sb("rows", [P, TOPK, NT, ROW])
        w1f = sb("w1f", [P, F])
        w2f = sb("w2f", [P, F])
        w1h, w1l = sb("w1h", [P, E * F], F16), sb("w1l", [P, E * F], F16)
        w2h, w2l = sb("w2h", [P, E * F], F16), sb("w2l", [P, E * F], F16)
        BW = F + D
        HI, LO = 0, 32
        bias = sb("bias", [P, E * BW], F16)
        bias_f = sb("bias_f", [LO + 1, BW])
        bias_t = sb("bias_t", [LO + 1, BW], F16)
        slot_x = sb("slot_x", [P, UNROLL, D])
        slot_meta = sb("slot_meta", [P, J, 2])
        slot_xT = sb("slot_xT", [P, 2, 2 * P], F16)
        h = sb("h", [P, 2, F])
        hh, hl = sb("hh", [P, UNROLL, F], F16), sb("hl", [P, UNROLL, F], F16)
        y = sb("y", [P, J, ROW])
        ya, yb = x_in, x_res
        stats2 = sb("stats2", [P, TB, 6])
        moments2 = sb("moments2", [P, TB, 2])
        rstd2 = sb("rstd2", [P, TB])
        res = probs[:, 0:2 * S].rearrange("p (i t d) -> p i t d", i=2, t=TB)

        bank = [ctx.enter_context(nc.psum_tensor(f"bank{i}", [P, 512], F32)) for i in range(8)]
        A0, A1, S01, S2, S3, T0, T1, O = bank
        score = [S01[:, 0:P], S01[:, P:3 * P], S2[:, 0:3 * P], S3[:, 0:4 * P]]
        route = T1
        psT, psH, psY = (A0, A1), (S2, S3), (T0, T1)

        const_ready = sem("const_ready")
        ones_ready = sem("ones_ready")
        w_loaded = sem("w_loaded")
        small_loaded = sem("small_loaded")
        x_in_loaded = sem("x_in_loaded")
        x_res_loaded = sem("x_res_loaded")
        ew_loaded = sem("ew_loaded")
        prefilled = sem("prefilled")
        wT_psum, wT_ready = sem("wT_psum"), sem("wT_ready")
        m_psum, m_ready = sem("m_psum"), sem("m_ready")
        xT_psum, xT_ready = sem("xT_psum"), sem("xT_ready")
        g_psum, g_ready = sem("g_psum"), sem("g_ready")
        v_psum, v_ready = sem("v_psum"), sem("v_ready")
        scores_psum, negmax_ready = sem("scores_psum"), sem("negmax_ready")
        rowmax_ready = sem("rowmax_ready")
        probs_ready = sem("probs_ready")
        pT_psum, pT_act, pT_dve = sem("pT_psum"), sem("pT_act"), sem("pT_dve")
        attn_psum, attn_read = sem("attn_psum"), sem("attn_read")
        dve_step = sem("dve_step")
        xn_ready, xnT_psum, xnT_ready = sem("xn_ready"), sem("xnT_psum"), sem("xnT_ready")
        halves_ready, rows_copied = sem("halves_ready"), sem("rows_copied")
        x1b_ready = sem("x1b_ready")
        logits_psum, logits_read = sem("logits_psum"), sem("logits_read")
        chosen_ready = sem("chosen_ready")
        route_psum, route_read = sem("route_psum"), sem("route_read")
        egap_ready, gap_ready = sem("egap_ready"), sem("gap_ready")
        dispatch_ready = sem("dispatch_ready")
        dispatched = [sem(f"dispatched{g}") for g in range(len(GROUPS))]
        ws_ready = sem("ws_ready")
        wh_ready, wl_ready = sem("wh_ready"), sem("wl_ready")
        slot_loaded = [sem(f"slot_loaded{s}") for s in range(UNROLL)]
        meta_loaded = sem("meta_loaded")
        wait_held = sem("wait_held")
        slotT_psum, slotT_ready = sem("slotT_psum"), sem("slotT_ready")
        h_psum, gelu_ready, h_split = sem("h_psum"), sem("gelu_ready"), sem("h_split")
        hh_ready = sem("hh_ready")
        y_psum, y_ready = sem("y_psum"), sem("y_ready")
        y_returned = [sem(f"y_returned{g}") for g in range(len(GROUPS))]
        pair_loaded, pair_used = sem("pair_loaded"), sem("pair_used")
        res_ready, stored = sem("res_ready"), [sem(f"stored{i}") for i in range(2)]

        NCONST = 12
        UNITS = 3
        UNIT = [(0, 1), (2,), (3,)]
        block = ctx.enter_context(nc.Block())

        emb_t = emb.rearrange("b (t p) d -> b p t d", p=P)
        out_t = out.rearrange("b (t p) d -> b p t d", p=P)

        def at(x, b, n):
            return bass.ds(b * n, n)

        @block.sync
        def _(sp):
            def batch_loads(b, first=False):
                if not first:
                    sp.wait_ge(xT_psum, b)
                sp.dma_start(x_in[:], emb_t[b] if first else
                             emb_t[bass.ds(b, 1)].rearrange("a p t d -> (a p) t d")).then_inc(x_in_loaded, 16)
                if first:
                    sp.dma_start(wq[:], W_Q).then_inc(w_loaded, 16)
                    sp.dma_start(wk[:], W_K).then_inc(w_loaded, 16)
                    sp.dma_start(wv[:], W_V).then_inc(w_loaded, 16)
                    sp.dma_start(gw[:], gate_w).then_inc(small_loaded, 16)
                    sp.dma_start(gb[:], gate_b.rearrange("(a e) -> a e", a=1).broadcast_to([P, E])).then_inc(small_loaded, 16)
                    sp.dma_start(lng[:], ln_g.rearrange("(a e) -> a e", a=1).broadcast_to([P, D])).then_inc(small_loaded, 16)
                    sp.dma_start(lnb[:], ln_b.rearrange("(a e) -> a e", a=1).broadcast_to([P, D])).then_inc(small_loaded, 16)
                if not first:
                    sp.wait_ge(attn_read, b)
                sp.dma_start(x_res[:], emb_t[b] if first else
                             emb_t[bass.ds(b, 1)].rearrange("a p t d -> (a p) t d")).then_inc(x_res_loaded, 16)
                if not first:
                    sp.wait_ge(wl_ready, 3 * b)
                sp.dma_start(w1f[:], w1[bass.ds(b, 1)].rearrange("a p f -> (a p) f")).then_inc(ew_loaded, 16)
                sp.dma_start(w2f[:].rearrange("p (c d) -> p c d", c=FC),
                             w2[bass.ds(b, 1)].rearrange("a (c p) d -> p (a c) d", p=P)).then_inc(ew_loaded, 16)
                for r in (HI, LO):
                    sp.dma_start(bias_f[r:r + 1, 0:F], b1[bass.ds(b, 1)]).then_inc(ew_loaded, 16)
                    sp.dma_start(bias_f[r:r + 1, F:BW], b2[bass.ds(b, 1)]).then_inc(ew_loaded, 16)
                if first:
                    sp.wait_ge(const_ready, NCONST)
                sp.dma_start(slots[bass.ds(b * (PREFILL * P), PREFILL * P), :].rearrange("(j p) w -> p j w", p=P),
                             y[:, bass.ds(b * PREFILL, PREFILL), :]).then_inc(prefilled, 16)

            batch_loads(0, first=True)
            with sp.Fori(1, B) as b:
                batch_loads(b)

            for g in range(len(GROUPS)):
                sp.wait_ge(dispatched[g], 16 * TOPK * GROUPS[g] * TB)
                i0, i1 = group_first[g] // UNROLL, (group_first[g] + group_tiles[g]) // UNROLL

                def slot_loads(i, first=False):
                    if not first:
                        sp.wait_ge(meta_loaded, 16 * i)
                    sp.dma_start(slot_meta[:, bass.ds(i * UNROLL, UNROLL), :],
                                 slots[bass.ds(i * (UNROLL * P), UNROLL * P), GATE:ROW]
                                 .rearrange("(j p) w -> p j w", p=P)).then_inc(meta_loaded, 16)
                    first_slot = i * (UNROLL * P) if first else sp.snap(i * (UNROLL * P))
                    for s in range(UNROLL):
                        if not first:
                            sp.wait_ge(slotT_psum, i * UNROLL + (s - UNROLL + 1))
                            sp.sem_inc(wait_held, 1)
                        sp.dma_start(slot_x[:, s, :], slots[bass.ds(first_slot + s * P, P), 0:D]).then_inc(slot_loaded[s], 16)

                if i0 == 0:
                    slot_loads(0, first=True)
                    i0 = 1
                with sp.Fori(i0, i1) as i:
                    slot_loads(i)

            for g in range(len(GROUPS)):
                sp.wait_ge(y_returned[g], 16 * group_tiles[g])
                for b in range(group_b0[g], group_b0[g] + GROUPS[g]):
                    if b:
                        sp.wait_ge(pair_used, b)
                    for k, buf in ((0, ya), (1, yb)):
                        r0 = k * N + b * S
                        sp.dma_start(buf[:], returned[r0:r0 + S, :].rearrange("(t p) d -> p t d", p=P)).then_inc(pair_loaded, 16)
            for i in range(2):
                sp.wait_ge(stored[i], 16 * (B // 2))

        @block.tensor
        def _(pe):
            def transpose_x(b):
                pe.wait_ge(x_in_loaded, (b + 1) * 16)
                if not isinstance(b, int) or b:
                    pe.wait_ge(v_ready, b)
                for t in range(TB):
                    m = nc.tensor.transpose(A0[:, t * P:(t + 1) * P], x_in[:, t, :], ident[:])
                m.then_inc(xT_psum, 1)

            def project_g(b):
                pe.wait_ge(xT_ready, b + 1)
                nc.tensor.matmul(A0[:], mqk[:], xT[:], start=True, stop=True).then_inc(g_psum, 1)

            def project_v(b):
                pe.wait_ge(g_ready, b + 1)
                for t in range(TB):
                    m = nc.tensor.matmul(A0[:, t * P:(t + 1) * P], xT[:, t * P:(t + 1) * P], wv[:], start=True, stop=True)
                m.then_inc(v_psum, 1)

            def scores(b):
                pe.wait_ge(g_ready, b + 1)
                if not isinstance(b, int) or b:
                    pe.wait_ge(probs_ready, b * UNITS)
                for u in range(UNITS):
                    for i in UNIT[u]:
                        nc.tensor.matmul(score[i], gT[:, i * P:(i + 1) * P], xT[:, 0:(i + 1) * P], start=True, stop=False)
                        m = nc.tensor.matmul(score[i][:, i * P:(i + 1) * P], ident_b[:], mask[:], start=False, stop=True)
                    m.then_inc(scores_psum, 1)

            def transpose_probs(b, u):
                bk = (T0, T1, T0)[u]
                pe.wait_ge(probs_ready, b * UNITS + (u + 1))
                if u == 2:
                    pe.wait_ge(pT_act, b * 2 + 1)
                elif u == 0:
                    if not isinstance(b, int) or b:
                        pe.wait_ge(pT_act, b * 2)
                elif not isinstance(b, int) or b:
                    pe.wait_ge(pT_dve, b)
                o0 = OFF[UNIT[u][0]]
                for i in UNIT[u]:
                    for j in range(i + 1):
                        o = OFF[i] + j * P
                        m = nc.tensor.transpose(bk[:, o - o0:o - o0 + P], probs[:, o:o + P], ident[:])
                m.then_inc(pT_psum, 1)

            def weigh_values(b, u):
                if u == 1:
                    pe.wait_ge(pT_dve, b + 1)
                else:
                    pe.wait_ge(pT_act, b * 2 + (1 if u == 0 else 2))
                if u == 0:
                    pe.wait_ge(v_ready, b + 1)
                    if not isinstance(b, int) or b:
                        pe.wait_ge(attn_read, b)
                for i in UNIT[u]:
                    for j in range(i + 1):
                        o = OFF[i] + j * P
                        m = nc.tensor.matmul(O[:, i * P:(i + 1) * P], probsT[:, o:o + P], v[:, j, :],
                                             start=(j == 0), stop=(j == i))
                if u == UNITS - 1:
                    m.then_inc(attn_psum, 1)

            def transpose_xn(b):
                pe.wait_ge(xn_ready, b + 1)
                if not isinstance(b, int) or b:
                    pe.wait_ge(logits_read, b)
                for t in range(TB):
                    m = nc.tensor.transpose(A1[:, t * P:(t + 1) * P], xn[:, t, :], ident[:])
                m.then_inc(xnT_psum, 1)

            def gate(b):
                pe.wait_ge(xnT_ready, b + 1)
                for t in range(TB):
                    m = nc.tensor.matmul(A1[:, t * E:(t + 1) * E], xnT[:, t * P:(t + 1) * P], gw[:], start=True, stop=True)
                m.then_inc(logits_psum, 1)

            def step(b, first=False, last=False):
                if not last:
                    transpose_x(b + 1)
                if not first:
                    transpose_xn(b - 1)
                if not last:
                    project_g(b + 1)
                if not first:
                    gate(b - 1)
                transpose_probs(b, 0)
                transpose_probs(b, 1)
                weigh_values(b, 0)
                transpose_probs(b, 2)
                weigh_values(b, 1)
                weigh_values(b, 2)
                if not last:
                    project_v(b + 1)
                    scores(b + 1)

            def prefix_sums(g):
                last_b = group_b0[g] + GROUPS[g]
                pe.wait_ge(chosen_ready, last_b)
                pe.wait_ge(pT_dve, min(last_b + 2, B))
                t0, n = group_b0[g] * TB, GROUPS[g] * TB
                picked = chosen[:, :, t0:t0 + n, :].rearrange("p k t e -> p k (t e)")
                w = TOPK * n * E
                halves = (T1, O)
                if g:
                    pe.wait_ge(attn_read, last_b)
                else:
                    pe.wait_ge(attn_read, last_b + 2)
                nc.tensor.matmul(halves[0][:, 0:w].rearrange("p (k c) -> p k c", k=TOPK), before[:], picked, start=True, stop=True)
                nc.tensor.matmul(halves[1][:, 0:w].rearrange("p (k c) -> p k c", k=TOPK), ones_h[:], picked, start=True, stop=True).then_inc(route_psum, 1)

            pe.wait_ge(const_ready, NCONST)
            pe.wait_ge(w_loaded, 48)
            nc.tensor.transpose(A1[:, 0:P], wq[:], ident[:])
            nc.tensor.transpose(A1[:, P:2 * P], wk[:], ident[:]).then_inc(wT_psum, 1)
            transpose_x(0)
            pe.wait_ge(wT_ready, 1)
            nc.tensor.matmul(A1[:, 2 * P:3 * P], wqkT[:, 0:P], wqkT[:, P:2 * P], start=True, stop=True).then_inc(m_psum, 1)
            pe.wait_ge(m_ready, 1)
            pe.wait_ge(small_loaded, 64)
            project_g(0)
            project_v(0)
            scores(0)

            ROUTE_AT = group_b0[1] + 2
            step(0, first=True)
            with pe.Fori(1, ROUTE_AT) as b:
                step(b)
            prefix_sums(0)
            with pe.Fori(ROUTE_AT, B - 1) as b:
                step(b)
            step(B - 1, last=True)
            transpose_xn(B - 1)
            gate(B - 1)
            prefix_sums(1)

            pe.wait_ge(wl_ready, 3 * B)
            pe.wait_ge(wh_ready, 4 * B)
            pe.wait_ge(route_read, 2)
            pe.wait_ge(logits_read, B)

            def transpose_slots(i, s):
                j = i * UNROLL + s
                pe.wait_ge(slot_loaded[s], (i + 1) * 16)
                if not isinstance(j, int) or j >= 2:
                    pe.wait_ge(slotT_ready, j - 1)
                src = slot_x[:, s, :].bitcast(F16)
                dst = psT[s % 2][:, 0:P].bitcast(F16)
                for k in range(2):
                    m = nc.tensor.transpose(dst[:, k * P:(k + 1) * P], src[:, k * D:(k + 1) * D], ident_h[:])
                m.then_inc(slotT_psum, 1)

            def expand(i, s, e):
                j = i * UNROLL + s
                pe.wait_ge(slotT_ready, j + 1)
                if not isinstance(j, int) or j >= 2:
                    pe.wait_ge(gelu_ready, j - 1)
                xh, xl = slot_xT[:, s % 2, 0:P], slot_xT[:, s % 2, P:2 * P]
                for c in range(FC):
                    o = psH[s % 2][:, c * P:(c + 1) * P]
                    at_c = bass.ds(e * F + c * P, P)
                    nc.tensor.matmul(o, w1h[:, at_c], xh, start=True, stop=False)
                    nc.tensor.matmul(o, w1h[:, at_c], xl, start=False, stop=False)
                    nc.tensor.matmul(o, w1l[:, at_c], xh, start=False, stop=False)
                    m = nc.tensor.matmul(o, bias[:, bass.ds(e * BW + c * P, P)], ones_h[:], start=False, stop=True)
                m.then_inc(h_psum, 1)

            def contract(j, s, e):
                pe.wait_ge(h_split, j + 1)
                if not isinstance(j, int) or j >= 2:
                    pe.wait_ge(y_ready, j - 1)
                o = psY[s % 2][:, 0:D]
                for c in range(FC):
                    at_c = bass.ds(e * F + c * D, D)
                    a, b_ = hh[:, s, c * P:(c + 1) * P], hl[:, s, c * P:(c + 1) * P]
                    nc.tensor.matmul(o, a, w2h[:, at_c], start=(c == 0), stop=False)
                    nc.tensor.matmul(o, a, w2l[:, at_c], start=False, stop=False)
                    nc.tensor.matmul(o, b_, w2h[:, at_c], start=False, stop=False)
                nc.tensor.matmul(o, ones_h[:], bias[:, bass.ds(e * BW + F, D)], start=False, stop=True).then_inc(y_psum, 1)

            def expert_numbers(i):
                return [pe.value_load(expert_of[0:1, bass.ds(i * UNROLL + k, 1)], min_val=0, max_val=E - 1)
                        for k in range(UNROLL + LAG)]

            def body(i):
                e = expert_numbers(i)
                for s in range(UNROLL):
                    transpose_slots(i, s)
                    if not isinstance(i, int) or s >= LAG:
                        contract(i * UNROLL + s - LAG, (s - LAG) % UNROLL, e[s])
                    expand(i, s, e[s + LAG])

            body(0)
            with pe.Fori(1, J // UNROLL) as i:
                body(i)
            e = expert_numbers(J // UNROLL - 0) if False else None
            for s in range(LAG):
                j = J - LAG + s
                contract(j, j % UNROLL, pe.value_load(expert_of[0:1, j + LAG:j + LAG + 1], min_val=0, max_val=E - 1))

        @block.scalar
        def _(act):
            def copy_g(b):
                act.wait_ge(g_psum, b + 1)
                nc.scalar.activation(gT[:], A0[:], ACT.Copy).then_inc(g_ready, 1)

            def copy_v(b):
                act.wait_ge(v_psum, b + 1)
                nc.scalar.activation(v[:].rearrange("p t d -> p (t d)"), A0[:], ACT.Copy).then_inc(v_ready, 1)

            def copy_xnT(b):
                act.wait_ge(xnT_psum, b + 1)
                nc.scalar.activation(xnT[:], A1[:], ACT.Copy).then_inc(xnT_ready, 1)

            def copy_probsT(b, u):
                act.wait_ge(pT_psum, b * UNITS + (u + 1))
                a, n = OFF[UNIT[u][0]], OFF[UNIT[u][-1] + 1] - OFF[UNIT[u][0]]
                nc.scalar.activation(probsT[:, a:a + n], T0[:, 0:n], ACT.Copy).then_inc(pT_act, 1)

            def exponentials(b):
                for u in range(UNITS):
                    act.wait_ge(negmax_ready, b * UNITS + (u + 1))
                    for i in UNIT[u]:
                        col = bass.ds(b * TB + i, 1)
                        m = nc.scalar.activation(probs[:, OFF[i]:OFF[i + 1]], score[i], ACT.Exp,
                                                 bias=negmax[:, col], scale=SCALE, accum_out=rowsum[:, col])
                    m.then_inc(probs_ready, 1)

            def weights_high(b):
                act.wait_ge(ew_loaded, b * 96 + 96)
                for w in (w1f[:], w2f[:], bias_f[LO:LO + 1, :]):
                    m = nc.scalar.activation(w, w, ACT.Copy, scale=WSCALE)
                m.then_inc(ws_ready, 1)
                act.wait_ge(ws_ready, b + 1)
                if not isinstance(b, int) or b:
                    act.wait_ge(wl_ready, b * 3)
                for high, w in ((w1h[:, bass.ds(b * F, F)], w1f[:]), (w2h[:, bass.ds(b * F, F)], w2f[:]),
                                (bias_t[LO:LO + 1, :], bias_f[LO:LO + 1, :])):
                    nc.scalar.activation(high, w, ACT.Copy).then_inc(wh_ready, 1)
                nc.scalar.activation(bias[HI:HI + 1, bass.ds(b * BW, BW)], bias_f[HI:HI + 1, :], ACT.Copy,
                                     scale=WSCALE).then_inc(wh_ready, 1)

            def step(b, first=False, last=False):
                if not first:
                    copy_xnT(b - 1)
                if not last:
                    copy_g(b + 1)
                copy_probsT(b, 0)
                copy_probsT(b, 2)
                if not last:
                    copy_v(b + 1)
                    exponentials(b + 1)
                weights_high(b)

            def gate_exp(g):
                t0, n = group_b0[g] * TB, GROUPS[g] * TB
                act.wait_ge(gap_ready, g + 1)
                nc.scalar.activation(egap[:, t0:t0 + n], gap[:, t0:t0 + n], ACT.Exp,
                                     scale=1.0 / TEMPERATURE).then_inc(egap_ready, 1)

            act.wait_ge(const_ready, NCONST)
            act.wait_ge(wT_psum, 1)
            nc.scalar.activation(wqkT[:], A1[:, 0:2 * P], ACT.Copy).then_inc(wT_ready, 1)
            act.wait_ge(m_psum, 1)
            nc.scalar.activation(mqk[:], A1[:, 2 * P:3 * P], ACT.Copy).then_inc(m_ready, 1)
            copy_g(0)
            copy_v(0)
            exponentials(0)
            step(0, first=True)
            ROUTE_AT = group_b0[1] + 2
            with act.Fori(1, ROUTE_AT) as b:
                step(b)
            gate_exp(0)
            with act.Fori(ROUTE_AT, B - 1) as b:
                step(b)
            step(B - 1, last=True)
            copy_xnT(B - 1)
            gate_exp(1)

            def body(i):
                for s in range(UNROLL):
                    j = i * UNROLL + s
                    act.wait_ge(slotT_psum, j + 1)
                    if not isinstance(j, int) or j >= 2:
                        act.wait_ge(h_psum, j - 1)
                    nc.scalar.activation(slot_xT[:, s % 2, :], psT[s % 2][:, 0:P].bitcast(F16), ACT.Copy).then_inc(slotT_ready, 1)
                    act.wait_ge(h_psum, j + 1)
                    if not isinstance(j, int) or j >= 2:
                        act.wait_ge(h_split, j - 1)
                    nc.scalar.activation(h[:, s % 2, :], psH[s % 2][:], ACT.Gelu, scale=1.0 / WSCALE).then_inc(gelu_ready, 1)

            body(0)
            with act.Fori(1, J // UNROLL) as i:
                body(i)
            for b in range(B):
                act.wait_ge(res_ready, b + 1)
                act.dma_start(out_t[b], res[:, b % 2]).then_inc(stored[b % 2], 16)

        @block.vector
        def _(dve):
            chain = [0]

            def link(ins):
                chain[0] += 1
                ins.then_inc(dve_step, 1)
                dve.wait_ge(dve_step, chain[0])

            def copy_xT(b):
                dve.wait_ge(xT_psum, b + 1)
                nc.vector.tensor_copy(xT[:], A0[:]).then_inc(xT_ready, 1)

            def maxima(b):
                for u in range(UNITS):
                    dve.wait_ge(scores_psum, b * UNITS + (u + 1))
                    for i in UNIT[u]:
                        m = nc.vector.reduce_max(rowmax[:, bass.ds(b * TB + i, 1)], score[i], AX.X)
                    m.then_inc(rowmax_ready, 1)
                    dve.wait_ge(rowmax_ready, b * UNITS + (u + 1))
                    cols = bass.ds(b * TB + UNIT[u][0], len(UNIT[u]))
                    nc.vector.tensor_scalar(negmax[:, cols], rowmax[:, cols], -SCALE, None, ALU.mult).then_inc(negmax_ready, 1)

            def copy_probsT(b):
                dve.wait_ge(pT_psum, b * UNITS + 2)
                a, n = OFF[2], OFF[3] - OFF[2]
                nc.vector.tensor_copy(probsT[:, a:a + n], T1[:, 0:n]).then_inc(pT_dve, 1)

            def settle(ins=None):
                dve.drain()

            def residual(b):
                lk = settle
                dve.wait_ge(attn_psum, b + 1)
                lk(nc.vector.reciprocal(rinv[:], rowsum[:, bass.ds(b * TB, TB)]))
                dve.wait_ge(x_res_loaded, (b + 1) * 16)
                for t in range(TB):
                    m = nc.vector.scalar_tensor_tensor(out=z[:, t, :], in0=O[:, t * P:(t + 1) * P], scalar=rinv[:, t:t + 1],
                                                       in1=x_res[:, t, :],
                                                       op0=ALU.mult, op1=ALU.add)
                m.then_inc(attn_read, 1)

            def norm_stats(lk, src, st, mo, rs):
                for t in range(TB):
                    m = nc.vector.bn_stats(st[:, t, :], src[:, t, :])
                lk(m)
                for t in range(TB):
                    m = nc.vector.bn_aggr(mo[:, t, :], st[:, t, :])
                lk(m)
                v3 = var[:].rearrange("p (t a) -> p t a", a=1)
                lk(nc.vector.tensor_scalar(v3, mo[:, :, 1:2], EPS, None, ALU.add))
                lk(nc.vector.tensor_scalar(rs[:].bitcast(I32), var[:].bitcast(I32), -0.5, RSQRT_MAGIC, ALU.mult, ALU.add))
                for _ in range(NEWTON):
                    lk(nc.vector.tensor_tensor(square[:], rs[:], rs[:], ALU.mult))
                    lk(nc.vector.scalar_tensor_tensor(out=square[:], in0=square[:], scalar=-0.5, in1=var[:], op0=ALU.mult, op1=ALU.mult))
                    lk(nc.vector.scalar_tensor_tensor(out=rs[:], in0=square[:], scalar=1.5, in1=rs[:], op0=ALU.add, op1=ALU.mult))

            def norm(b):
                lk = settle
                dve.wait_ge(attn_read, b + 1)
                norm_stats(lk, z, stats, moments, rstd)
                if not isinstance(b, int) or b:
                    dve.wait_ge(xnT_psum, b)
                    dve.wait_ge(x1b_ready, b)
                for t in range(TB):
                    m = nc.vector.tensor_scalar(xn[:, t, :], z[:, t, :], moments[:, t, 0:1], rstd[:, t:t + 1],
                                                ALU.subtract, ALU.mult)
                m.then_inc(xn_ready, 1)
                dve.wait_ge(xn_ready, b + 1)
                if not isinstance(b, int) or b:
                    dve.wait_ge(rows_copied, b * 2)
                xh, xl = x_halves[:, :, 0:D], x_halves[:, :, D:2 * D]
                nc.vector.tensor_copy(xh, xn[:]).then_inc(halves_ready, 1)
                dve.wait_ge(halves_ready, b * 2 + 1)
                nc.vector.tensor_tensor(xl, xn[:], xh, ALU.subtract).then_inc(halves_ready, 1)

            def choose(b):
                lk = settle
                dve.wait_ge(logits_psum, b + 1)
                nc.vector.tensor_tensor(logits[:], A1[:, 0:TB * E].rearrange("p (t e) -> p t e", t=TB),
                                        gb[:].rearrange("p (a e) -> p a e", a=1).broadcast_to([P, TB, E]), ALU.add).then_inc(logits_read, 1)
                settle()
                for t in range(TB):
                    m = nc.vector.max(top[:, t, :], logits[:, t, :])
                lk(m)
                for t in range(TB):
                    m = nc.vector.max_index(topi[:, t, :], top[:, t, :], logits[:, t, :])
                lk(m)
                lk(nc.vector.tensor_copy(topf[:], topi[:, :, 0:TOPK]))
                lk(nc.vector.tensor_tensor(gap[:, bass.ds(b * TB, TB)].rearrange("p (t a) -> p t a", a=1),
                                           top[:, :, 1:2], top[:, :, 0:1], ALU.subtract))
                for k in range(TOPK):
                    m = nc.vector.tensor_tensor(
                        chosen[:, k, bass.ds(b * TB, TB), :],
                        expert_id[:].rearrange("p (a e) -> p a e", a=1).broadcast_to([P, TB, E]),
                        topf[:, :, k:k + 1].broadcast_to([P, TB, E]), ALU.is_equal)
                    if k == 0:
                        lk(m)
                m.then_inc(chosen_ready, 1)

            def step(b, first=False, last=False):
                if not last:
                    copy_xT(b + 1)
                copy_probsT(b)
                residual(b)
                if not last:
                    maxima(b + 1)
                norm(b)
                if not first:
                    choose(b - 1)

            def assign(g):
                t0, n = group_b0[g] * TB, GROUPS[g] * TB
                m, w = TOPK * n, TOPK * n * E
                nc.vector.tensor_scalar(gap[:, t0:t0 + n], gap[:, t0:t0 + n], 1.0, None, ALU.mult).then_inc(gap_ready, 1)
                dve.wait_ge(route_psum, g + 1)
                pre, tot = T1[:, 0:w], O[:, 0:w]
                flat = lambda x: x[:, 0:m, :].rearrange("p m e -> p (m e)")
                link(nc.vector.tensor_copy(flat(total), tot))
                for e in range(E):
                    ins = nc.vector.tensor_tensor_scan(running[:, 0:m, e], ones[:, 0:m], total[:, 0:m, e], 0.0,
                                                       ALU.mult, ALU.add)
                link(ins)
                link(nc.vector.tensor_scalar(padded_i[:], running[:, m - 1, :], float(P - 1), None, ALU.add))
                link(nc.vector.tensor_scalar(padded_i[:], padded_i[:], -P, None, ALU.bitwise_and))
                link(nc.vector.tensor_copy(padded[:], padded_i[:]))
                link(nc.vector.tensor_tensor_scan(ends[:], ones[:, 0:E], padded[:], 0.0, ALU.mult, ALU.add))
                link(nc.vector.tensor_tensor(base[:], ends[:], padded[:], ALU.subtract))
                link(nc.vector.tensor_tensor(flat(place), pre, flat(running), ALU.add))
                link(nc.vector.tensor_tensor(flat(place), flat(place), flat(total), ALU.subtract))
                link(nc.vector.tensor_tensor(place[:, 0:m, :], place[:, 0:m, :],
                                             base[:].rearrange("p (a e) -> p a e", a=1).broadcast_to([P, m, E]), ALU.add))
                for k in range(TOPK):
                    ins = nc.vector.tensor_tensor(place[:, k * n:(k + 1) * n, :], place[:, k * n:(k + 1) * n, :],
                                                  chosen[:, k, t0:t0 + n, :], ALU.mult)
                link(ins)
                link(nc.vector.tensor_reduce(slot_f[:, 0:m], place[:, 0:m, :], AX.X, ALU.add))
                link(nc.vector.tensor_scalar(slot_of[:, g, 0:m], slot_f[:, 0:m], float(group_first[g] * P), None, ALU.add))
                nt = group_tiles[g]
                link(nc.vector.tensor_tensor(passed[:, 0:nt, :],
                                             tile_start[:, 0:nt].rearrange("p (t a) -> p t a", a=1).broadcast_to([1, nt, E]),
                                             ends[0:1, :].rearrange("p (a e) -> p a e", a=1).broadcast_to([1, nt, E]), ALU.is_ge))
                link(nc.vector.tensor_reduce(passed_n[:, 0:nt], passed[:, 0:nt, :], AX.X, ALU.add))
                j0 = LAG + group_first[g]
                link(nc.vector.tensor_scalar(expert_of[:, j0:j0 + nt], passed_n[:, 0:nt], float(E - 1), None, ALU.min))
                dve.wait_ge(egap_ready, g + 1)
                link(nc.vector.tensor_scalar(p1[:, t0:t0 + n], egap[:, t0:t0 + n], WSCALE, WSCALE, ALU.mult, ALU.add))
                link(nc.vector.reciprocal(p1[:, t0:t0 + n], p1[:, t0:t0 + n]))
                col = lambda k: rows[:, k, t0:t0 + n, GATE]
                nc.vector.tensor_copy(col(0), p1[:, t0:t0 + n])
                link(nc.vector.tensor_tensor(col(1), p1[:, t0:t0 + n], egap[:, t0:t0 + n], ALU.mult))
                nc.vector.tensor_scalar(gap[:, t0:t0 + n], egap[:, t0:t0 + n], 1.0, None, ALU.mult).then_inc(dispatch_ready, 1)
                dve.wait_ge(dispatch_ready, g + 1)
                nc.vector.memset(rinv[0:1, 0:1], 0.0).then_inc(route_read, 1)

            nc.vector.memset(ones[:], 1.0).then_inc(ones_ready, 1)
            dve.wait_ge(ones_ready, 1)
            dve.wait_ge(small_loaded, 64)
            dve.wait_ge(const_ready, NCONST)
            copy_xT(0)
            maxima(0)
            ROUTE_AT = group_b0[1] + 2
            step(0, first=True)
            with dve.Fori(1, ROUTE_AT) as b:
                step(b)
            assign(0)
            with dve.Fori(ROUTE_AT, B - 1) as b:
                step(b)
            step(B - 1, last=True)
            choose(B - 1)
            assign(1)

            def split(i, s):
                j = i * UNROLL + s
                dve.wait_ge(gelu_ready, j + 1)
                nc.vector.tensor_copy(hh[:, s, :], h[:, s % 2, :]).then_inc(hh_ready, 1)
                dve.wait_ge(hh_ready, j + 1)
                nc.vector.tensor_tensor(hl[:, s, :], h[:, s % 2, :], hh[:, s, :], ALU.subtract).then_inc(h_split, 1)

            def weigh(j, s):
                dve.wait_ge(y_psum, j + 1)
                nc.vector.tensor_scalar(y[:, bass.ds(j, 1), 0:D].rearrange("p a d -> p (a d)"), psY[s % 2][:, 0:D],
                                        slot_meta[:, bass.ds(j, 1), 0:1].rearrange("p a d -> p (a d)"), None, ALU.mult).then_inc(y_ready, 1)

            def body(i):
                dve.wait_ge(meta_loaded, (i + 1) * 16)
                for s in range(UNROLL):
                    if not isinstance(i, int) or s >= LAG:
                        weigh(i * UNROLL + s - LAG, (s - LAG) % UNROLL)
                    split(i, s)

            body(0)
            with dve.Fori(1, J // UNROLL) as i:
                body(i)
            for s in range(LAG):
                weigh(J - LAG + s, (J - LAG + s) % UNROLL)

            for b in range(B):
                if b:
                    dve.wait_ge(res_ready, b)
                dve.wait_ge(pair_loaded, 32 * (b + 1))
                link(nc.vector.tensor_tensor(z[:], ya[:], yb[:], ALU.add))
                norm_stats(link, z, stats, moments, rstd)
                for t in range(TB):
                    ins = nc.vector.tensor_scalar(z[:, t, :], z[:, t, :], moments[:, t, 0:1], rstd[:, t:t + 1],
                                                  ALU.subtract, ALU.mult)
                link(ins)
                link(nc.vector.tensor_tensor(z[:], z[:], lng[:].rearrange("p (a d) -> p a d", a=1).broadcast_to([P, TB, D]), ALU.mult))
                nc.vector.tensor_tensor(z[:], z[:], x1b[:, b * TB:(b + 1) * TB, :], ALU.add).then_inc(pair_used, 1)
                dve.wait_ge(pair_used, b + 1)
                norm_stats(link, z, stats2, moments2, rstd2)
                if b >= 2:
                    dve.wait_ge(stored[b % 2], 16 * (b // 2))
                for t in range(TB):
                    ins = nc.vector.tensor_scalar(res[:, b % 2, t, :], z[:, t, :], moments2[:, t, 0:1], rstd2[:, t:t + 1],
                                                  ALU.subtract, ALU.mult)
                ins.then_inc(res_ready, 1)

        @block.gpsimd
        def _(pool):
            made = sem("made")
            g = nc.gpsimd
            g.memset(ident[:], 0.0).then_inc(made, 1)
            g.memset(mask[:], 0.0).then_inc(made, 1)
            g.memset(before[:], 1.0).then_inc(made, 1)
            g.memset(ones_h[:], 1.0).then_inc(const_ready, 1)
            pool.wait_ge(made, 3)
            g.affine_select(out=ident[:], in_=ident[:], compare_op=ALU.not_equal, fill=1.0, base=0,
                            pattern=[[-1, P]], channel_multiplier=1).then_inc(const_ready, 1)
            g.affine_select(out=mask[:], in_=mask[:], compare_op=ALU.is_ge, fill=MASKED, base=0,
                            pattern=[[-1, P]], channel_multiplier=1).then_inc(const_ready, 1)
            g.affine_select(out=before[:], in_=before[:], compare_op=ALU.is_gt, fill=0.0, base=0,
                            pattern=[[1, P]], channel_multiplier=-1).then_inc(const_ready, 1)
            pool.wait_ge(const_ready, 4)
            g.tensor_copy(ident_h[:], ident[:]).then_inc(const_ready, 1)
            g.tensor_copy(ident_b[:], ident[:]).then_inc(const_ready, 1)
            g.iota(expert_id[:], [[1, E]], base=0, channel_multiplier=0, allow_small_or_imprecise_dtypes=True).then_inc(const_ready, 1)
            g.iota(tile_start[:], [[P, max(group_tiles)]], base=0, channel_multiplier=0,
                   allow_small_or_imprecise_dtypes=True).then_inc(const_ready, 1)
            g.iota(rows[:, :, :, BACK].bitcast(I32), [[N, TOPK], [P, NT]], base=0, channel_multiplier=1).then_inc(const_ready, 1)
            g.memset(y[:], 0.0).then_inc(made, 1)
            pool.wait_ge(made, 4)
            g.iota(y[:, :, BACK].bitcast(I32), [[P, J]], base=TOPK * N, channel_multiplier=1).then_inc(const_ready, 1)
            g.memset(expert_of[:], 0).then_inc(const_ready, 1)
            g.memset(bias[:], 0.0).then_inc(const_ready, 1)

            def weights_low(b):
                pool.wait_ge(wh_ready, b * 4 + 4)
                g.tensor_tensor(w1l[:, bass.ds(b * F, F)], w1f[:], w1h[:, bass.ds(b * F, F)], ALU.subtract).then_inc(wl_ready, 1)
                g.tensor_tensor(w2l[:, bass.ds(b * F, F)], w2f[:], w2h[:, bass.ds(b * F, F)], ALU.subtract).then_inc(wl_ready, 1)
                pool.wait_ge(wl_ready, b * 3 + 2)
                g.tensor_tensor(bias[LO:LO + 1, bass.ds(b * BW, BW)], bias_f[LO:LO + 1, :], bias_t[LO:LO + 1, :],
                                ALU.subtract).then_inc(wl_ready, 1)
                pool.wait_ge(wl_ready, b * 3 + 3)

            def keep(b):
                pool.wait_ge(xn_ready, b + 1)
                tiles = bass.ds(b * TB, TB)
                g.tensor_tensor(x1b[:, tiles, :], xn[:], lnb[:].rearrange("p (a d) -> p a d", a=1).broadcast_to([P, TB, D]),
                                ALU.add).then_inc(x1b_ready, 1)
                pool.wait_ge(halves_ready, b * 2 + 2)
                for k in range(TOPK):
                    g.tensor_copy(rows[:, k, tiles, 0:D], x_halves[:].bitcast(F32)).then_inc(rows_copied, 1)

            def dispatch(gr):
                pool.wait_ge(dispatch_ready, gr + 1)
                pool.wait_ge(prefilled, 16 * B if gr else 16 * -(-group_tiles[0] // PREFILL))
                pool.wait_ge(rows_copied, TOPK * (B if gr else last_a + 1))
                n = GROUPS[gr] * TB
                for t in range(n):
                    for k in range(TOPK):
                        c = k * n + t
                        g.indirect_dma_start(slots, bass.IndirectOffsetOnAxis(ap=slot_of[:, gr, c:c + 1], axis=0),
                                             rows[:, k, group_b0[gr] * TB + t, :], None).then_inc(dispatched[gr], 16)

            pool.wait_ge(small_loaded, 64)
            last_a = group_b0[1] + 1
            with pool.Fori(0, last_a + 1) as b:
                weights_low(b)
                keep(b)
            dispatch(0)
            pool.wait_ge(dispatched[0], 16 * TOPK * GROUPS[0] * TB)
            with pool.Fori(last_a + 1, B) as b:
                weights_low(b)
                keep(b)
            dispatch(1)
            for gr in range(len(GROUPS)):
                for j in range(group_first[gr], group_first[gr] + group_tiles[gr]):
                    pool.wait_ge(y_ready, j + 1)
                    g.indirect_dma_start(returned, bass.IndirectOffsetOnAxis(ap=slot_meta[:, j, 1:2].bitcast(U32), axis=0),
                                         y[:, j, 0:D], None).then_inc(y_returned[gr], 16)


_INS = ["L0_attn_embeddings", "L0_attn_W_Q", "L0_attn_W_K", "L0_attn_W_V", "L0_ffn_gate_w", "L0_ffn_gate_b",
        "L0_ffn_w1", "L0_ffn_b1", "L0_ffn_w2", "L0_ffn_b2", "L0_ffn_ln_g", "L0_ffn_ln_b"]


def kernel(**inputs):
    import numpy as _np
    import concourse.bacc as _bacc
    from concourse import mybir as _mybir
    from concourse.bass_utils import run_bass_kernel_spmd as _run

    nc = _bacc.Bacc("TRN2", target_bir_lowering=False, num_devices=1)
    arrays, args = {}, []
    for name in _INS:
        a = _np.ascontiguousarray(inputs[name])
        arrays[f"in_{name}_dram"] = a
        args.append(nc.dram_tensor(f"in_{name}_dram", a.shape, _mybir.dt.from_np(a.dtype), kind="ExternalInput").ap())
    shape = arrays["in_L0_attn_embeddings_dram"].shape
    args.append(nc.dram_tensor("out_0_dram", shape, _mybir.dt.float32, kind="ExternalOutput").ap())
    moe_block(nc, *args)
    r = _run(nc, [arrays], core_ids=[0])
    return r.results[0]["out_0_dram"]
```

```python
from contextlib import ExitStack

import concourse.bass as bass
from concourse import mybir

F32 = mybir.dt.float32
F16 = mybir.dt.float16
BF16 = mybir.dt.bfloat16
I32 = mybir.dt.int32
U32 = mybir.dt.uint32
U8 = mybir.dt.uint8
ALU = mybir.AluOpType
ACT = mybir.ActivationFunctionType
AX = mybir.AxisListType

P = 128
GROUPS = (3, 5)
UNROLL = 8
LAG = 2
TEMPERATURE = 0.9
EPS = 1e-5
WSCALE = 64.0
MASKED = -1e30
RSQRT_MAGIC = float(0x5F3759DF)


def moe_block(nc, emb, W_Q, W_K, W_V, gate_w, gate_b, w1, b1, w2, b2, ln_g, ln_b, out):
    B, S, D = emb.shape
    E, _, F = w1.shape
    TB = S // P
    NT = B * TB
    N = NT * P
    FC = F // P
    TOPK = 2
    SCALE = float(D) ** -0.5
    assert D == P and TB == 4 and sum(GROUPS) == B and E == 8

    group_tiles, group_first, group_b0 = [], [], []
    for g, nb in enumerate(GROUPS):
        need = nb * TB * TOPK + E - 1
        group_first.append(sum(group_tiles))
        group_b0.append(sum(GROUPS[:g]))
        group_tiles.append((need + UNROLL - 1) // UNROLL * UNROLL)
    J = sum(group_tiles)
    PREFILL = J // B
    assert J % B == 0
    ROW = D + 2
    GATE, BACK = D, D + 1

    slots = nc.dram_tensor("slots", [J * P, ROW], F32, kind="Internal").ap()
    returned = nc.dram_tensor("returned", [TOPK * N + J * P, D], F32, kind="Internal").ap()

    ctx = ExitStack()
    with ctx:
        def sb(name, shape, dt=F32):
            return ctx.enter_context(nc.sbuf_tensor(name, shape, dt))

        def sem(name):
            return ctx.enter_context(nc.semaphore(name))

        ident = sb("ident", [P, P])
        ident_h = sb("ident_h", [P, P], F16)
        ident_b = sb("ident_b", [P, P], BF16)
        mask = sb("mask", [P, P], BF16)
        before = sb("before", [P, P], F16)
        ones_h = sb("ones_h", [P, P], F16)
        ones = sb("ones", [P, 64])
        expert_id = sb("expert_id", [P, E])
        wscale = sb("wscale", [P, 1])
        tile_start = sb("tile_start", [1, max(group_tiles)])
        wq, wk, wv = (sb(n, [P, D]) for n in ("wq", "wk", "wv"))
        wqkT = sb("wqkT", [P, 2 * D])
        mqk = sb("mqk", [P, D])
        x_in = sb("x_in", [P, TB, D])
        x_res = sb("x_res", [P, TB, D])
        xT = sb("xT", [P, S])
        gT = sb("gT", [P, S])
        v = sb("v", [P, TB, D])
        OFF = [P * i * (i + 1) // 2 for i in range(TB + 1)]
        probs = sb("probs", [P, OFF[TB]])
        probsT = sb("probsT", [P, OFF[TB]])
        negmax = sb("negmax", [P, NT])
        rowsum = sb("rowsum", [P, NT])
        rinv = sb("rinv", [P, TB])
        z = sb("z", [P, TB, D])
        stats = sb("stats", [P, TB, 6])
        moments = sb("moments", [P, TB, 2])
        rstd = sb("rstd", [P, TB])
        var, square = sb("var", [P, TB]), sb("square", [P, TB])
        xn = sb("xn", [P, TB, D])
        xnT = sb("xnT", [P, S])
        x1 = sb("x1", [P, NT, D])
        gw = sb("gw", [P, E])
        gb = sb("gb", [P, E])
        lng = sb("lng", [P, D])
        lnb = sb("lnb", [P, D])
        logits = sb("logits", [P, TB, E])
        top = sb("top", [P, TB, E])
        topi = sb("topi", [P, TB, E], U32)
        gap = sb("gap", [P, NT])
        egap = sb("egap", [P, NT])
        p1 = sb("p1", [P, NT])
        chosen = sb("chosen", [P, TOPK, NT, E], F16)
        NG = max(GROUPS) * TB * TOPK
        total = sb("total", [P, NG, E])
        running = sb("running", [P, NG, E])
        place = sb("place", [P, NG, E])
        padded_i = sb("padded_i", [P, E], I32)
        padded = sb("padded", [P, E])
        ends = sb("ends", [P, E])
        base = sb("base", [P, E])
        slot_f = sb("slot_f", [P, NG])
        slot_of = sb("slot_of", [P, len(GROUPS), NG], U32)
        HB = 4
        passed = sb("passed", [1, max(group_tiles), E])
        passed_n = sb("passed_n", [1, max(group_tiles)])
        expert_of = sb("expert_of", [1, LAG + J + 2], I32)
        rows = sb("rows", [P, TOPK, NT, ROW])
        W = 2 * F
        wf = sb("wf", [P, W])
        PART = 2 * W + P
        experts = sb("experts", [P, E * PART], F16)
        BW, LO = F + D, 32
        bias_f = sb("bias_f", [LO + E, BW])
        bias_t = sb("bias_t", [LO + E, BW], F16)
        bias = sb("bias", [P, BW], F16)
        y_low = sb("y_low", [P, HB, D])
        slot_x = sb("slot_x", [P, HB, D])
        slot_meta = sb("slot_meta", [P, J, 2])
        slot_xT = sb("slot_xT", [P, 2, 2 * P], F16)
        h = sb("h", [P, 2, F])
        hh, hl = sb("hh", [P, HB, F], F16), sb("hl", [P, HB, F], F16)
        y = sb("y", [P, J, ROW])
        ya, yb = x_in, x_res
        stats2 = sb("stats2", [P, TB, 6])
        moments2 = sb("moments2", [P, TB, 2])
        rstd2 = sb("rstd2", [P, TB])
        res = probs[:, 0:2 * S].rearrange("p (i t d) -> p i t d", i=2, t=TB)

        bank = [ctx.enter_context(nc.psum_tensor(f"bank{i}", [P, 512], F32)) for i in range(8)]
        A0, A1, S01, S2, S3, T0, T1, O = bank
        score = [S01[:, 0:P], S01[:, P:3 * P], S2[:, 0:3 * P], S3[:, 0:4 * P]]
        route = T1
        psT, psH, psY = (A0, A1), (S2, S3), (T0, T1, O, S01)

        const_ready = sem("const_ready")
        ones_ready = sem("ones_ready")
        w_loaded = sem("w_loaded")
        small_loaded = sem("small_loaded")
        x_in_loaded = sem("x_in_loaded")
        x_res_loaded = sem("x_res_loaded")
        ew_loaded = sem("ew_loaded")
        prefilled = sem("prefilled")
        wT_psum, wT_ready = sem("wT_psum"), sem("wT_ready")
        m_psum, m_ready = sem("m_psum"), sem("m_ready")
        xT_psum, xT_ready = sem("xT_psum"), sem("xT_ready")
        g_psum, g_ready = sem("g_psum"), sem("g_ready")
        v_psum, v_ready = sem("v_psum"), sem("v_ready")
        scores_psum, negmax_ready = sem("scores_psum"), sem("negmax_ready")
        probs_ready = sem("probs_ready")
        pT_psum, pT_act, pT_dve = sem("pT_psum"), sem("pT_act"), sem("pT_dve")
        attn_psum, attn_read = sem("attn_psum"), sem("attn_read")
        dve_step = sem("dve_step")
        xn_ready, xnT_psum, xnT_ready = sem("xn_ready"), sem("xnT_psum"), sem("xnT_ready")
        halves_ready, x1_kept = sem("halves_ready"), sem("x1_kept")
        x1b_ready = sem("x1b_ready")
        rows_copied = [sem(f"rows_copied{g}") for g in range(len(GROUPS))]
        logits_psum, logits_read = sem("logits_psum"), sem("logits_read")
        chosen_ready = sem("chosen_ready")
        route_psum, route_read = sem("route_psum"), sem("route_read")
        egap_ready = sem("egap_ready")
        dispatch_ready = sem("dispatch_ready")
        dispatched = [sem(f"dispatched{g}") for g in range(len(GROUPS))]
        ws_ready = sem("ws_ready")
        wh_ready, wl_ready = sem("wh_ready"), sem("wl_ready")
        bias_loaded, bias_ready = sem("bias_loaded"), sem("bias_ready")
        slot_loaded = [sem(f"slot_loaded{s}") for s in range(HB)]
        meta_loaded = sem("meta_loaded")
        wait_held = sem("wait_held")
        slotT_psum, slotT_ready = sem("slotT_psum"), sem("slotT_ready")
        h_psum, gelu_ready, h_split = sem("h_psum"), sem("gelu_ready"), sem("h_split")
        hh_ready = sem("hh_ready")
        y_psum, y_low_ready, y_ready = sem("y_psum"), sem("y_low_ready"), sem("y_ready")
        y_returned = [sem(f"y_returned{g}") for g in range(len(GROUPS))]
        pair_loaded, pair_used = sem("pair_loaded"), sem("pair_used")
        res_ready, stored = sem("res_ready"), [sem(f"stored{i}") for i in range(2)]

        NCONST = 14
        UNITS = 3
        UNIT = [(0, 1), (2,), (3,)]
        block = ctx.enter_context(nc.Block())

        emb_t = emb.rearrange("b (t p) d -> b p t d", p=P)
        out_t = out.rearrange("b (t p) d -> b p t d", p=P)

        def chunks(e, low):
            return experts[:, bass.ds(e * PART, 2 * W)].rearrange("p (c k d) -> p c k d", k=2, d=P)[:, :, low, :]

        @block.sync
        def _(sp):
            def batch(x, b):
                return x[b] if isinstance(b, int) else x[bass.ds(b, 1)].rearrange("a p t d -> (a p) t d")

            def copies(b, group):
                tiles = bass.ds(b * TB, TB)
                sp.wait_ge(xn_ready, b + 1)
                sp.dma_start(x1[:, tiles, :], xn[:]).then_inc(x1_kept, 16)
                sp.wait_ge(halves_ready, b + 1)
                sp.dma_start(rows[:, 1, tiles, 0:D], rows[:, 0, tiles, 0:D]).then_inc(rows_copied[group], 16)

            def load_x_in(b):
                sp.wait_ge(xT_psum, b)
                sp.dma_start(x_in[:], batch(emb_t, b)).then_inc(x_in_loaded, 16)

            def load_x_res(b):
                sp.wait_ge(attn_read, b)
                sp.dma_start(x_res[:], batch(emb_t, b)).then_inc(x_res_loaded, 16)

            def beside_step(b, group):
                load_x_in(b + 2)
                copies(b - 1, group)
                load_x_res(b + 1)

            sp.dma_start(x_in[:], emb_t[0]).then_inc(x_in_loaded, 16)
            sp.dma_start(wq[:], W_Q).then_inc(w_loaded, 16)
            sp.dma_start(wk[:], W_K).then_inc(w_loaded, 16)
            sp.dma_start(wv[:], W_V).then_inc(w_loaded, 16)
            sp.dma_start(x_res[:], emb_t[0]).then_inc(x_res_loaded, 16)
            sp.dma_start(gw[:], gate_w).then_inc(small_loaded, 16)
            for row, src, n in ((gb, gate_b, E), (lng, ln_g, D), (lnb, ln_b, D)):
                sp.dma_start(row[:], src.rearrange("(a e) -> a e", a=1).broadcast_to([P, n])).then_inc(small_loaded, 16)
            for r in (0, LO):
                sp.dma_start(bias_f[r:r + E, 0:F], b1).then_inc(bias_loaded, 16)
                sp.dma_start(bias_f[r:r + E, F:BW], b2).then_inc(bias_loaded, 16)
            load_x_in(1)
            load_x_in(2)
            load_x_res(1)
            with sp.Fori(1, GROUPS[0] + 1) as b:
                beside_step(b, 0)
            with sp.Fori(GROUPS[0] + 1, B - 2) as b:
                beside_step(b, 1)
            copies(B - 3, 1)
            load_x_res(B - 1)
            copies(B - 2, 1)
            copies(B - 1, 1)

            for g in range(len(GROUPS)):
                sp.wait_ge(dispatched[g], 16 * TOPK * GROUPS[g] * TB)
                i0, i1 = group_first[g] // UNROLL, (group_first[g] + group_tiles[g]) // UNROLL

                def slot_loads(i, first=False):
                    if not first:
                        sp.wait_ge(meta_loaded, 16 * i)
                    sp.dma_start(slot_meta[:, bass.ds(i * UNROLL, UNROLL), :],
                                 slots[bass.ds(i * (UNROLL * P), UNROLL * P), GATE:ROW]
                                 .rearrange("(j p) w -> p j w", p=P)).then_inc(meta_loaded, 16)
                    first_slot = i * (UNROLL * P) if first else sp.snap(i * (UNROLL * P))
                    for s in range(UNROLL):
                        if not first:
                            sp.wait_ge(slotT_psum, i * UNROLL + (s - HB + 1))
                            sp.sem_inc(wait_held, 1)
                        elif s >= HB:
                            sp.wait_ge(slotT_psum, s - HB + 1)
                        sp.dma_start(slot_x[:, s % HB, :], slots[bass.ds(first_slot + s * P, P), 0:D]).then_inc(slot_loaded[s % HB], 16)

                if i0 == 0:
                    slot_loads(0, first=True)
                    i0 = 1
                with sp.Fori(i0, i1) as i:
                    slot_loads(i)

            for g in range(len(GROUPS)):
                sp.wait_ge(y_returned[g], 16 * group_tiles[g])
                for b in range(group_b0[g], group_b0[g] + GROUPS[g]):
                    if b:
                        sp.wait_ge(pair_used, b)
                    for k, buf in ((0, ya), (1, yb)):
                        r0 = k * N + b * S
                        sp.dma_start(buf[:], returned[r0:r0 + S, :].rearrange("(t p) d -> p t d", p=P)).then_inc(pair_loaded, 16)
            for i in range(2):
                sp.wait_ge(stored[i], 16 * (B // 2))

        @block.tensor
        def _(pe):
            def transpose_x(b):
                pe.wait_ge(x_in_loaded, (b + 1) * 16)
                if not isinstance(b, int) or b:
                    pe.wait_ge(v_ready, b)
                for t in range(TB):
                    m = nc.tensor.transpose(A0[:, t * P:(t + 1) * P], x_in[:, t, :], ident[:])
                m.then_inc(xT_psum, 1)

            def project_g(b):
                pe.wait_ge(xT_ready, b + 1)
                nc.tensor.matmul(A0[:], mqk[:], xT[:], start=True, stop=True).then_inc(g_psum, 1)

            def project_v(b):
                pe.wait_ge(g_ready, b + 1)
                for t in range(TB):
                    m = nc.tensor.matmul(A0[:, t * P:(t + 1) * P], xT[:, t * P:(t + 1) * P], wv[:], start=True, stop=True)
                m.then_inc(v_psum, 1)

            def scores(b):
                pe.wait_ge(g_ready, b + 1)
                if not isinstance(b, int) or b:
                    pe.wait_ge(probs_ready, b * UNITS)
                for u in range(UNITS):
                    for i in UNIT[u]:
                        nc.tensor.matmul(score[i], gT[:, i * P:(i + 1) * P], xT[:, 0:(i + 1) * P], start=True, stop=False)
                        m = nc.tensor.matmul(score[i][:, i * P:(i + 1) * P], ident_b[:], mask[:], start=False, stop=True)
                    m.then_inc(scores_psum, 1)

            def transpose_probs(b, u):
                bk = (T0, T1, T0)[u]
                pe.wait_ge(probs_ready, b * UNITS + (u + 1))
                if u == 2:
                    pe.wait_ge(pT_act, b * 2 + 1)
                elif u == 0:
                    if not isinstance(b, int) or b:
                        pe.wait_ge(pT_act, b * 2)
                elif not isinstance(b, int) or b:
                    pe.wait_ge(pT_dve, b)
                o0 = OFF[UNIT[u][0]]
                for i in UNIT[u]:
                    for j in range(i + 1):
                        o = OFF[i] + j * P
                        m = nc.tensor.transpose(bk[:, o - o0:o - o0 + P], probs[:, o:o + P], ident[:])
                m.then_inc(pT_psum, 1)

            def weigh_values(b, u):
                if u == 1:
                    pe.wait_ge(pT_dve, b + 1)
                else:
                    pe.wait_ge(pT_act, b * 2 + (1 if u == 0 else 2))
                if u == 0:
                    pe.wait_ge(v_ready, b + 1)
                    if not isinstance(b, int) or b:
                        pe.wait_ge(attn_read, b)
                for i in UNIT[u]:
                    for j in range(i + 1):
                        o = OFF[i] + j * P
                        m = nc.tensor.matmul(O[:, i * P:(i + 1) * P], probsT[:, o:o + P], v[:, j, :],
                                             start=(j == 0), stop=(j == i))
                if u == UNITS - 1:
                    m.then_inc(attn_psum, 1)

            def transpose_xn(b):
                pe.wait_ge(xn_ready, b + 1)
                if not isinstance(b, int) or b:
                    pe.wait_ge(logits_read, b)
                for t in range(TB):
                    m = nc.tensor.transpose(A1[:, t * P:(t + 1) * P], xn[:, t, :], ident[:])
                m.then_inc(xnT_psum, 1)

            def gate(b):
                pe.wait_ge(xnT_ready, b + 1)
                for t in range(TB):
                    m = nc.tensor.matmul(A1[:, t * E:(t + 1) * E], xnT[:, t * P:(t + 1) * P], gw[:], start=True, stop=True)
                m.then_inc(logits_psum, 1)

            def step(b, first=False, last=False, routed=False):
                if not last:
                    transpose_x(b + 1)
                transpose_probs(b, 0)
                if routed:
                    pe.wait_ge(route_read, 1)
                transpose_probs(b, 1)
                if not last:
                    project_g(b + 1)
                weigh_values(b, 0)
                transpose_probs(b, 2)
                weigh_values(b, 1)
                if not first:
                    transpose_xn(b - 1)
                weigh_values(b, 2)
                if not first:
                    gate(b - 1)
                if not last:
                    project_v(b + 1)
                    scores(b + 1)

            def prefix_sums(g):
                last_b = group_b0[g] + GROUPS[g]
                pe.wait_ge(chosen_ready, last_b)
                pe.wait_ge(pT_dve, min(last_b + 2, B))
                t0, n = group_b0[g] * TB, GROUPS[g] * TB
                picked = chosen[:, :, t0:t0 + n, :].rearrange("p k t e -> p k (t e)")
                w = TOPK * n * E
                halves = (T1, O)
                if g:
                    pe.wait_ge(attn_read, last_b)
                else:
                    pe.wait_ge(attn_read, last_b + 2)
                nc.tensor.matmul(halves[0][:, 0:w].rearrange("p (k c) -> p k c", k=TOPK), before[:], picked, start=True, stop=True)
                nc.tensor.matmul(halves[1][:, 0:w].rearrange("p (k c) -> p k c", k=TOPK), ones_h[:], picked, start=True, stop=True).then_inc(route_psum, 1)

            pe.wait_ge(const_ready, NCONST)
            pe.wait_ge(w_loaded, 48)
            nc.tensor.transpose(A1[:, 0:P], wq[:], ident[:])
            nc.tensor.transpose(A1[:, P:2 * P], wk[:], ident[:]).then_inc(wT_psum, 1)
            transpose_x(0)
            pe.wait_ge(wT_ready, 1)
            nc.tensor.matmul(A1[:, 2 * P:3 * P], wqkT[:, 0:P], wqkT[:, P:2 * P], start=True, stop=True).then_inc(m_psum, 1)
            pe.wait_ge(m_ready, 1)
            pe.wait_ge(small_loaded, 64)
            project_g(0)
            project_v(0)
            scores(0)

            ROUTE_AT = group_b0[1] + 2
            step(0, first=True)
            with pe.Fori(1, ROUTE_AT) as b:
                step(b)
            prefix_sums(0)
            with pe.Fori(ROUTE_AT, B - 1) as b:
                step(b, routed=True)
            step(B - 1, last=True)
            transpose_xn(B - 1)
            gate(B - 1)
            prefix_sums(1)

            pe.wait_ge(wl_ready, E)
            pe.wait_ge(wh_ready, E)
            pe.wait_ge(bias_ready, 5)
            pe.wait_ge(dispatch_ready, 2)
            pe.wait_ge(logits_read, B)

            def transpose_slots(i, s):
                pe.wait_ge(slot_loaded[s % HB], i * (UNROLL // HB * 16) + (s // HB + 1) * 16)
                src = slot_x[:, s % HB, :].bitcast(F16)
                dst = psT[s % 2][:, 0:P].bitcast(F16)
                for k in range(2):
                    m = nc.tensor.transpose(dst[:, k * P:(k + 1) * P], src[:, k * D:(k + 1) * D], ident_h[:])
                m.then_inc(slotT_psum, 1)

            def of_expert(col, n, offset):
                return experts[:].bitcast(U8)[:, 2 * col:][:, bass.ds(offset, 2 * n)].bitcast(F16)

            def expand(i, s, e):
                pe.wait_ge(slotT_ready, i * UNROLL + (s + 1))
                xh, xl = slot_xT[:, s % 2, 0:P], slot_xT[:, s % 2, P:2 * P]
                picked = of_expert(2 * W, P, e)
                for c in range(FC):
                    o = psH[s % 2][:, c * P:(c + 1) * P]
                    high, low = of_expert(2 * c * P, P, e), of_expert((2 * c + 1) * P, P, e)
                    nc.tensor.matmul(o, high, xh, start=True, stop=False)
                    nc.tensor.matmul(o, high, xl, start=False, stop=False)
                    nc.tensor.matmul(o, low, xh, start=False, stop=False)
                    m = nc.tensor.matmul(o, bias[:, c * P:(c + 1) * P], picked, start=False, stop=True)
                m.then_inc(h_psum, 1)

            def contract(j, s, e):
                pe.wait_ge(h_split, j + 1)
                both, main = psY[s % HB][:, 0:2 * D], psY[s % HB][:, 0:D]
                for c in range(FC):
                    col, rows_c = 2 * (F + c * D), slice(c * P, (c + 1) * P)
                    if c == FC - 1:
                        nc.tensor.matmul(main, of_expert(2 * W, P, e), bias[:, F:BW], start=False, stop=False)
                        nc.tensor.matmul(main, hl[:, s % HB, rows_c], of_expert(col, D, e), start=False, stop=False)
                    m = nc.tensor.matmul(both, hh[:, s % HB, rows_c], of_expert(col, 2 * D, e), start=(c == 0), stop=(c == FC - 1))
                    if c < FC - 1:
                        nc.tensor.matmul(main, hl[:, s % HB, rows_c], of_expert(col, D, e), start=False, stop=False)
                m.then_inc(y_psum, 1)

            def expert_numbers(first, n):
                _, e = nc.values_load_multi_w_load_instructions(expert_of[0:1, bass.ds(first, n)],
                                                                engines=[mybir.EngineType.PE], min_val=0, max_val=E - 1,
                                                                skip_runtime_bounds_check_because="assign() computes 0 .. E - 1")
                return [pe.snap(x * (2 * PART)) for x in e]

            def body(i, last=False):
                e = expert_numbers(i * UNROLL, UNROLL + LAG)
                for s in range(UNROLL):
                    if s < UNROLL - 1:
                        transpose_slots(i, s + 1)
                    elif not last:
                        transpose_slots(i + 1, 0)
                    if not isinstance(i, int) or i or s >= LAG:
                        contract(i * UNROLL + s - LAG, (s - LAG) % UNROLL, e[s])
                    expand(i, s, e[s + LAG])

            transpose_slots(0, 0)
            body(0)
            with pe.Fori(1, J // UNROLL - 1) as i:
                body(i)
            body(J // UNROLL - 1, last=True)
            e = expert_numbers(J, LAG)
            for s in range(LAG):
                contract(J - LAG + s, (J - LAG + s) % UNROLL, e[s])

        @block.scalar
        def _(act):
            def copy_g(b):
                act.wait_ge(g_psum, b + 1)
                nc.scalar.activation(gT[:], A0[:], ACT.Copy).then_inc(g_ready, 1)

            def copy_v(b):
                act.wait_ge(v_psum, b + 1)
                nc.scalar.activation(v[:].rearrange("p t d -> p (t d)"), A0[:], ACT.Copy).then_inc(v_ready, 1)

            def copy_xnT(b):
                act.wait_ge(xnT_psum, b + 1)
                nc.scalar.activation(xnT[:], A1[:], ACT.Copy).then_inc(xnT_ready, 1)

            def copy_probsT(b, u):
                act.wait_ge(pT_psum, b * UNITS + (u + 1))
                a, n = OFF[UNIT[u][0]], OFF[UNIT[u][-1] + 1] - OFF[UNIT[u][0]]
                nc.scalar.activation(probsT[:, a:a + n], T0[:, 0:n], ACT.Copy).then_inc(pT_act, 1)

            def exponentials(b):
                for u in range(UNITS):
                    act.wait_ge(negmax_ready, b * UNITS + (u + 1))
                    for i in UNIT[u]:
                        col = bass.ds(b * TB + i, 1)
                        m = nc.scalar.activation(probs[:, OFF[i]:OFF[i + 1]], score[i], ACT.Exp,
                                                 bias=negmax[:, col], accum_out=rowsum[:, col])
                    m.then_inc(probs_ready, 1)

            def copy_xT(b):
                act.wait_ge(xT_psum, b + 1)
                nc.scalar.activation(xT[:], A0[:], ACT.Copy).then_inc(xT_ready, 1)

            def load_expert(e):
                if not isinstance(e, int) or e:
                    act.wait_ge(wl_ready, e)
                act.dma_start(wf[:, 0:F], w1[bass.ds(e, 1)].rearrange("a p f -> (a p) f")).then_inc(ew_loaded, 16)
                act.dma_start(wf[:, F:W].rearrange("p (c d) -> p c d", c=FC),
                             w2[bass.ds(e, 1)].rearrange("a (c p) d -> p (a c) d", p=P)).then_inc(ew_loaded, 16)

            def prefill(b):
                act.dma_start(slots[bass.ds(b * (PREFILL * P), PREFILL * P), :].rearrange("(j p) w -> p j w", p=P),
                             y[:, bass.ds(b * PREFILL, PREFILL), :]).then_inc(prefilled, 16)

            def weights_high(e):
                act.wait_ge(ws_ready, e + 1)
                nc.scalar.activation(chunks(e, 0), wf[:].rearrange("p (c d) -> p c d", d=P), ACT.Copy).then_inc(wh_ready, 1)

            def step(b, first=False, last=False):
                if not last:
                    copy_xT(b + 1)
                copy_probsT(b, 0)
                if not last:
                    copy_g(b + 1)
                if not first:
                    load_expert(b)
                prefill(b)
                copy_probsT(b, 2)
                if not first:
                    copy_xnT(b - 1)
                if not last:
                    copy_v(b + 1)
                    exponentials(b + 1)
                weights_high(b)

            def gate_exp(g):
                t0, n = group_b0[g] * TB, GROUPS[g] * TB
                act.wait_ge(chosen_ready, group_b0[g] + GROUPS[g])
                nc.scalar.activation(egap[:, t0:t0 + n], gap[:, t0:t0 + n], ACT.Exp,
                                     scale=1.0 / TEMPERATURE).then_inc(egap_ready, 1)

            load_expert(0)
            act.wait_ge(const_ready, NCONST)
            act.wait_ge(wT_psum, 1)
            nc.scalar.activation(wqkT[:], A1[:, 0:2 * P], ACT.Copy).then_inc(wT_ready, 1)
            act.wait_ge(m_psum, 1)
            nc.scalar.activation(mqk[:], A1[:, 2 * P:3 * P], ACT.Copy, scale=SCALE).then_inc(m_ready, 1)
            copy_xT(0)
            copy_g(0)
            copy_v(0)
            exponentials(0)
            step(0, first=True)
            ROUTE_AT = group_b0[1] + 2
            with act.Fori(1, ROUTE_AT) as b:
                step(b)
            gate_exp(0)
            with act.Fori(ROUTE_AT, B - 1) as b:
                step(b)
            step(B - 1, last=True)
            copy_xnT(B - 1)
            gate_exp(1)

            def copy_slots(j, s):
                act.wait_ge(slotT_psum, j + 1)
                nc.scalar.activation(slot_xT[:, s % 2, :], psT[s % 2][:, 0:P].bitcast(F16), ACT.Copy).then_inc(slotT_ready, 1)

            def gelu(j, s):
                act.wait_ge(h_psum, j + 1)
                nc.scalar.activation(h[:, s % 2, :], psH[s % 2][:], ACT.Gelu, scale=1.0 / WSCALE).then_inc(gelu_ready, 1)

            def weigh_low(j, s):
                nc.scalar.activation(y_low[:, s % HB, :], psY[s % HB][:, D:2 * D], ACT.Copy,
                                     scale=slot_meta[:, bass.ds(j, 1), 0:1].rearrange("p a d -> p (a d)")).then_inc(y_low_ready, 1)

            def body(i, last=False):
                act.wait_ge(meta_loaded, (i + 1) * 16)
                for s in range(UNROLL):
                    if s < UNROLL - 1 or not last:
                        copy_slots(i * UNROLL + (s + 1), s + 1)
                    gelu(i * UNROLL + s, s)
                    if not isinstance(i, int) or i or s >= LAG:
                        weigh_low(i * UNROLL + (s - LAG), (s - LAG) % UNROLL)

            copy_slots(0, 0)
            body(0)
            with act.Fori(1, J // UNROLL - 1) as i:
                body(i)
            body(J // UNROLL - 1, last=True)
            for s in range(LAG):
                act.wait_ge(y_psum, J - LAG + s + 1)
                weigh_low(J - LAG + s, (J - LAG + s) % UNROLL)
            for b in range(B):
                act.wait_ge(res_ready, b + 1)
                act.dma_start(out_t[b], res[:, b % 2]).then_inc(stored[b % 2], 16)

        @block.vector
        def _(dve):
            chain = [0]

            def link(ins):
                chain[0] += 1
                ins.then_inc(dve_step, 1)
                dve.wait_ge(dve_step, chain[0])

            def maxima(b):
                for u in range(UNITS):
                    dve.wait_ge(scores_psum, b * UNITS + (u + 1))
                    for i in UNIT[u]:
                        m = nc.vector.reduce_max(negmax[:, bass.ds(b * TB + i, 1)], score[i], AX.X, negate=True)
                    m.then_inc(negmax_ready, 1)

            def copy_probsT(b):
                dve.wait_ge(pT_psum, b * UNITS + 2)
                a, n = OFF[2], OFF[3] - OFF[2]
                nc.vector.tensor_copy(probsT[:, a:a + n], T1[:, 0:n]).then_inc(pT_dve, 1)

            def residual(b):
                dve.wait_ge(attn_psum, b + 1)
                nc.vector.reciprocal(rinv[:], rowsum[:, bass.ds(b * TB, TB)])
                dve.drain()
                dve.wait_ge(x_res_loaded, (b + 1) * 16)
                for t in range(TB):
                    m = nc.vector.scalar_tensor_tensor(out=z[:, t, :], in0=O[:, t * P:(t + 1) * P], scalar=rinv[:, t:t + 1],
                                                       in1=x_res[:, t, :], op0=ALU.mult, op1=ALU.add)
                m.then_inc(attn_read, 1)

            def rsqrt_step(i, r, variance, tmp):
                v = nc.vector
                if i == 0:
                    v.tensor_scalar(r.bitcast(I32), variance.bitcast(I32), -0.5, RSQRT_MAGIC, ALU.mult, ALU.add)
                elif i in (1, 5):
                    v.tensor_tensor(tmp, r, r, ALU.mult)
                elif i == 2:
                    v.tensor_tensor(tmp, tmp, variance, ALU.mult)
                elif i == 3:
                    v.scalar_tensor_tensor(out=tmp, in0=tmp, scalar=-10.0 / 3.0, in1=tmp, op0=ALU.add, op1=ALU.mult)
                elif i == 4:
                    v.scalar_tensor_tensor(out=r, in0=tmp, scalar=5.0, in1=r, op0=ALU.add, op1=ALU.mult)
                elif i == 6:
                    v.scalar_tensor_tensor(out=tmp, in0=tmp, scalar=-0.5 * 0.375 ** 3, in1=variance, op0=ALU.mult, op1=ALU.mult)
                else:
                    v.scalar_tensor_tensor(out=r, in0=tmp, scalar=1.5 * 0.375, in1=r, op0=ALU.add, op1=ALU.mult)

            def norm_and_choose(b, norm=True, choose=True):
                v = nc.vector
                c = b - 1
                tiles, ctiles = (bass.ds(x * TB, TB) for x in (b, c))
                if norm:
                    dve.wait_ge(attn_read, b + 1)
                    for t in range(TB):
                        v.bn_stats(stats[:, t, :], z[:, t, :])
                if choose:
                    dve.wait_ge(logits_psum, b)
                    v.tensor_tensor(logits[:], A1[:, 0:TB * E].rearrange("p (t e) -> p t e", t=TB),
                                    gb[:].rearrange("p (a e) -> p a e", a=1).broadcast_to([P, TB, E]), ALU.add).then_inc(logits_read, 1)
                dve.drain()
                if norm:
                    for t in range(TB):
                        v.bn_aggr(moments[:, t, :], stats[:, t, :])
                if choose:
                    for t in range(TB):
                        v.max(top[:, t, :], logits[:, t, :])
                dve.drain()
                if norm:
                    v.tensor_scalar(var[:].rearrange("p (t a) -> p t a", a=1), moments[:, :, 1:2], EPS, None, ALU.add)
                if choose:
                    for t in range(TB):
                        v.max_index(topi[:, t, :], top[:, t, :], logits[:, t, :])
                    v.tensor_tensor(gap[:, ctiles].rearrange("p (t a) -> p t a", a=1), top[:, :, 1:2], top[:, :, 0:1], ALU.subtract)
                dve.drain()
                if norm:
                    rsqrt_step(0, rstd[:], var[:], square[:])
                if choose:
                    for k in range(TOPK):
                        m = v.tensor_tensor(chosen[:, k, ctiles, :],
                                            expert_id[:].rearrange("p (a e) -> p a e", a=1).broadcast_to([P, TB, E]),
                                            topi[:, :, k:k + 1].broadcast_to([P, TB, E]), ALU.is_equal)
                    m.then_inc(chosen_ready, 1)
                if norm:
                    for i in range(1, 8):
                        dve.drain()
                        rsqrt_step(i, rstd[:], var[:], square[:])
                    dve.drain()
                    if not isinstance(b, int) or b:
                        dve.wait_ge(xnT_psum, b)
                        dve.wait_ge(x1_kept, b * 16)
                    for t in range(TB):
                        m = v.tensor_scalar(xn[:, t, :], z[:, t, :], moments[:, t, 0:1], rstd[:, t:t + 1],
                                            ALU.subtract, ALU.mult)
                    m.then_inc(xn_ready, 1)
                    dve.drain()
                    halves = rows[:].bitcast(F16)
                    v.tensor_copy(halves[:, 0, tiles, 0:D], xn[:])
                    dve.drain()
                    v.tensor_tensor(halves[:, 0, tiles, D:2 * D], xn[:], halves[:, 0, tiles, 0:D], ALU.subtract).then_inc(halves_ready, 1)

            def step(b, first=False, last=False):
                copy_probsT(b)
                residual(b)
                if not last:
                    maxima(b + 1)
                norm_and_choose(b, choose=not first)

            def split_biases():
                dve.wait_ge(bias_loaded, 64)
                v, low = nc.vector, slice(LO, LO + E)
                v.tensor_scalar(bias_f[low, :], bias_f[low, :], WSCALE, None, ALU.mult).then_inc(bias_ready, 1)
                v.tensor_scalar(bias[0:E, :], bias_f[0:E, :], WSCALE, None, ALU.mult).then_inc(bias_ready, 1)
                dve.wait_ge(bias_ready, 2)
                v.tensor_copy(bias_t[low, :], bias_f[low, :]).then_inc(bias_ready, 1)
                dve.wait_ge(bias_ready, 3)
                v.tensor_tensor(bias[low, :], bias_f[low, :], bias_t[low, :], ALU.subtract).then_inc(bias_ready, 2)

            def assign(g):
                t0, n = group_b0[g] * TB, GROUPS[g] * TB
                m, w = TOPK * n, TOPK * n * E
                dve.wait_ge(route_psum, g + 1)
                pre, tot = T1[:, 0:w], O[:, 0:w]
                flat = lambda x: x[:, 0:m, :].rearrange("p m e -> p (m e)")
                nc.vector.tensor_copy(flat(place), pre)
                link(nc.vector.tensor_copy(flat(total), tot))
                nc.vector.memset(rinv[0:1, 0:1], 0.0).then_inc(route_read, 1)
                for e in range(E):
                    ins = nc.vector.tensor_tensor_scan(running[:, 0:m, e], ones[:, 0:m], total[:, 0:m, e], 0.0,
                                                       ALU.mult, ALU.add)
                link(ins)
                link(nc.vector.tensor_scalar(padded_i[:], running[:, m - 1, :], float(P - 1), None, ALU.add))
                link(nc.vector.tensor_scalar(padded_i[:], padded_i[:], -P, None, ALU.bitwise_and))
                link(nc.vector.tensor_copy(padded[:], padded_i[:]))
                link(nc.vector.tensor_tensor_scan(ends[:], ones[:, 0:E], padded[:], 0.0, ALU.mult, ALU.add))
                link(nc.vector.tensor_tensor(base[:], ends[:], padded[:], ALU.subtract))
                link(nc.vector.tensor_tensor(flat(place), flat(place), flat(running), ALU.add))
                link(nc.vector.tensor_tensor(flat(place), flat(place), flat(total), ALU.subtract))
                link(nc.vector.tensor_tensor(place[:, 0:m, :], place[:, 0:m, :],
                                             base[:].rearrange("p (a e) -> p a e", a=1).broadcast_to([P, m, E]), ALU.add))
                for k in range(TOPK):
                    ins = nc.vector.tensor_tensor(place[:, k * n:(k + 1) * n, :], place[:, k * n:(k + 1) * n, :],
                                                  chosen[:, k, t0:t0 + n, :], ALU.mult)
                link(ins)
                link(nc.vector.tensor_reduce(slot_f[:, 0:m], place[:, 0:m, :], AX.X, ALU.add))
                link(nc.vector.tensor_scalar(slot_of[:, g, 0:m], slot_f[:, 0:m], float(group_first[g] * P), None, ALU.add))
                nt = group_tiles[g]
                link(nc.vector.tensor_tensor(passed[:, 0:nt, :],
                                             tile_start[:, 0:nt].rearrange("p (t a) -> p t a", a=1).broadcast_to([1, nt, E]),
                                             ends[0:1, :].rearrange("p (a e) -> p a e", a=1).broadcast_to([1, nt, E]), ALU.is_ge))
                link(nc.vector.tensor_reduce(passed_n[:, 0:nt], passed[:, 0:nt, :], AX.X, ALU.add))
                j0 = LAG + group_first[g]
                link(nc.vector.tensor_scalar(expert_of[:, j0:j0 + nt], passed_n[:, 0:nt], float(E - 1), None, ALU.min))
                dve.wait_ge(egap_ready, g + 1)
                link(nc.vector.tensor_scalar(p1[:, t0:t0 + n], egap[:, t0:t0 + n], WSCALE, WSCALE, ALU.mult, ALU.add))
                link(nc.vector.reciprocal(p1[:, t0:t0 + n], p1[:, t0:t0 + n]))
                col = lambda k: rows[:, k, t0:t0 + n, GATE]
                nc.vector.tensor_copy(col(0), p1[:, t0:t0 + n])
                link(nc.vector.tensor_tensor(col(1), p1[:, t0:t0 + n], egap[:, t0:t0 + n], ALU.mult))
                nc.vector.memset(rinv[0:1, 0:1], 0.0).then_inc(dispatch_ready, 1)

            nc.vector.memset(ones[:], 1.0).then_inc(ones_ready, 1)
            dve.wait_ge(ones_ready, 1)
            dve.wait_ge(small_loaded, 64)
            dve.wait_ge(const_ready, NCONST)
            maxima(0)
            ROUTE_AT = group_b0[1] + 2
            split_biases()
            step(0, first=True)
            with dve.Fori(1, ROUTE_AT) as b:
                step(b)
            assign(0)
            with dve.Fori(ROUTE_AT, B - 1) as b:
                step(b)
            step(B - 1, last=True)
            norm_and_choose(B, norm=False)
            assign(1)

            def split(i, s):
                dve.wait_ge(gelu_ready, i * UNROLL + (s + 1))
                nc.vector.tensor_copy(hh[:, s % HB, :], h[:, s % 2, :])
                dve.drain()
                nc.vector.tensor_tensor(hl[:, s % HB, :], h[:, s % 2, :], hh[:, s % HB, :], ALU.subtract).then_inc(h_split, 1)

            def weigh(j, s):
                tile = bass.ds(j, 1)
                flat = "p a d -> p (a d)"
                dve.wait_ge(y_low_ready, j + 1)
                nc.vector.scalar_tensor_tensor(out=y[:, tile, 0:D].rearrange(flat), in0=psY[s % HB][:, 0:D],
                                               scalar=slot_meta[:, tile, 0:1].rearrange(flat), in1=y_low[:, s % HB, :],
                                               op0=ALU.mult, op1=ALU.add).then_inc(y_ready, 1)

            def body(i):
                dve.wait_ge(meta_loaded, (i + 1) * 16)
                for s in range(UNROLL):
                    split(i, s)
                    if not isinstance(i, int) or i or s >= LAG:
                        weigh(i * UNROLL + (s - LAG), (s - LAG) % UNROLL)

            body(0)
            with dve.Fori(1, J // UNROLL) as i:
                body(i)
            for s in range(LAG):
                weigh(J - LAG + s, (J - LAG + s) % UNROLL)

            def norm_stats(src, st, mo, rs):
                for t in range(TB):
                    m = nc.vector.bn_stats(st[:, t, :], src[:, t, :])
                dve.drain()
                for t in range(TB):
                    m = nc.vector.bn_aggr(mo[:, t, :], st[:, t, :])
                dve.drain()
                nc.vector.tensor_scalar(var[:].rearrange("p (t a) -> p t a", a=1), mo[:, :, 1:2], EPS, None, ALU.add)
                for i in range(8):
                    dve.drain()
                    rsqrt_step(i, rs[:], var[:], square[:])
                dve.drain()

            for b in range(B):
                if b:
                    dve.wait_ge(res_ready, b)
                dve.wait_ge(pair_loaded, 32 * (b + 1))
                link(nc.vector.tensor_tensor(z[:], ya[:], yb[:], ALU.add))
                norm_stats(z, stats, moments, rstd)
                for t in range(TB):
                    ins = nc.vector.tensor_scalar(z[:, t, :], z[:, t, :], moments[:, t, 0:1], rstd[:, t:t + 1],
                                                  ALU.subtract, ALU.mult)
                link(ins)
                link(nc.vector.tensor_tensor(z[:], z[:], lng[:].rearrange("p (a d) -> p a d", a=1).broadcast_to([P, TB, D]), ALU.mult))
                if b == 0:
                    dve.wait_ge(x1b_ready, 1)
                nc.vector.tensor_tensor(z[:], z[:], x1[:, b * TB:(b + 1) * TB, :], ALU.add).then_inc(pair_used, 1)
                dve.wait_ge(pair_used, b + 1)
                norm_stats(z, stats2, moments2, rstd2)
                if b >= 2:
                    dve.wait_ge(stored[b % 2], 16 * (b // 2))
                for t in range(TB):
                    ins = nc.vector.tensor_scalar(res[:, b % 2, t, :], z[:, t, :], moments2[:, t, 0:1], rstd2[:, t:t + 1],
                                                  ALU.subtract, ALU.mult)
                ins.then_inc(res_ready, 1)

        @block.gpsimd
        def _(pool):
            made = sem("made")
            g = nc.gpsimd
            g.memset(ident[:], 0.0).then_inc(made, 1)
            g.memset(wscale[:], WSCALE).then_inc(const_ready, 1)
            g.memset(mask[:], 0.0).then_inc(made, 1)
            g.memset(before[:], 1.0).then_inc(made, 1)
            g.memset(ones_h[:], 1.0).then_inc(const_ready, 1)
            pool.wait_ge(made, 3)
            g.affine_select(out=ident[:], in_=ident[:], compare_op=ALU.not_equal, fill=1.0, base=0,
                            pattern=[[-1, P]], channel_multiplier=1).then_inc(const_ready, 1)
            g.affine_select(out=mask[:], in_=mask[:], compare_op=ALU.is_ge, fill=MASKED, base=0,
                            pattern=[[-1, P]], channel_multiplier=1).then_inc(const_ready, 1)
            g.affine_select(out=before[:], in_=before[:], compare_op=ALU.is_gt, fill=0.0, base=0,
                            pattern=[[1, P]], channel_multiplier=-1).then_inc(const_ready, 1)
            pool.wait_ge(const_ready, 5)
            g.tensor_copy(ident_h[:], ident[:]).then_inc(const_ready, 1)
            g.tensor_copy(ident_b[:], ident[:]).then_inc(const_ready, 1)
            g.iota(expert_id[:], [[1, E]], base=0, channel_multiplier=0, allow_small_or_imprecise_dtypes=True).then_inc(const_ready, 1)
            g.iota(tile_start[:], [[P, max(group_tiles)]], base=0, channel_multiplier=0,
                   allow_small_or_imprecise_dtypes=True).then_inc(const_ready, 1)
            g.iota(rows[:, :, :, BACK].bitcast(I32), [[N, TOPK], [P, NT]], base=0, channel_multiplier=1).then_inc(const_ready, 1)
            g.memset(y[:], 0.0).then_inc(made, 1)
            pool.wait_ge(made, 4)
            g.iota(y[:, :, BACK].bitcast(I32), [[P, J]], base=TOPK * N, channel_multiplier=1).then_inc(const_ready, 1)
            g.memset(expert_of[:], 0).then_inc(const_ready, 1)
            g.memset(bias[:], 0.0).then_inc(const_ready, 1)
            by_expert = experts[:].rearrange("p (e m) -> p e m", e=E)[:, :, 2 * W:PART]
            g.memset(by_expert, 0.0).then_inc(made, 1)
            pool.wait_ge(made, 5)
            g.affine_select(out=by_expert, in_=by_expert, compare_op=ALU.not_equal, fill=1.0, base=0,
                            pattern=[[-1, E], [0, P]], channel_multiplier=1).then_inc(made, 1)
            pool.wait_ge(made, 6)
            g.affine_select(out=by_expert, in_=by_expert, compare_op=ALU.not_equal, fill=1.0, base=-LO,
                            pattern=[[-1, E], [0, P]], channel_multiplier=1).then_inc(const_ready, 1)

            def split_weights(e):
                pool.wait_ge(ew_loaded, e * 32 + 32)
                g.tensor_tensor(wf[:], wf[:], wscale[:].broadcast_to([P, W]), ALU.mult).then_inc(ws_ready, 1)
                pool.wait_ge(wh_ready, e + 1)
                g.tensor_tensor(chunks(e, 1), wf[:].rearrange("p (c d) -> p c d", d=P), chunks(e, 0), ALU.subtract).then_inc(wl_ready, 1)

            def dispatch(gr, t0, t1):
                n = GROUPS[gr] * TB
                for t in range(t0, t1):
                    for k in range(TOPK):
                        c = k * n + t
                        g.indirect_dma_start(slots, bass.IndirectOffsetOnAxis(ap=slot_of[:, gr, c:c + 1], axis=0),
                                             rows[:, k, group_b0[gr] * TB + t, :], None).then_inc(dispatched[gr], 16)

            split_first = group_b0[1] + 2
            with pool.Fori(0, split_first) as e:
                split_weights(e)
            parts = E - split_first
            for i in range(parts):
                split_weights(split_first + i)
                if i == 0:
                    pool.wait_ge(dispatch_ready, 1)
                    pool.wait_ge(prefilled, 16 * -(-group_tiles[0] // PREFILL))
                    pool.wait_ge(rows_copied[0], 16 * GROUPS[0])
                n = GROUPS[0] * TB
                dispatch(0, n * i // parts, n * (i + 1) // parts)
            pool.wait_ge(dispatch_ready, 2)
            pool.wait_ge(prefilled, 16 * B)
            pool.wait_ge(rows_copied[1], 16 * GROUPS[1])
            dispatch(1, 0, GROUPS[1] * TB)
            pool.wait_ge(x1_kept, 16 * B)
            for b in range(B):
                tiles = slice(b * TB, (b + 1) * TB)
                ins = g.tensor_tensor(x1[:, tiles, :], x1[:, tiles, :], lnb[:].rearrange("p (a d) -> p a d", a=1).broadcast_to([P, TB, D]),
                                      ALU.add)
            ins.then_inc(x1b_ready, 1)
            for gr in range(len(GROUPS)):
                for j in range(group_first[gr], group_first[gr] + group_tiles[gr]):
                    pool.wait_ge(y_ready, j + 1)
                    g.indirect_dma_start(returned, bass.IndirectOffsetOnAxis(ap=slot_meta[:, j, 1:2].bitcast(U32), axis=0),
                                         y[:, j, 0:D], None).then_inc(y_returned[gr], 16)


_INS = ["L0_attn_embeddings", "L0_attn_W_Q", "L0_attn_W_K", "L0_attn_W_V", "L0_ffn_gate_w", "L0_ffn_gate_b",
        "L0_ffn_w1", "L0_ffn_b1", "L0_ffn_w2", "L0_ffn_b2", "L0_ffn_ln_g", "L0_ffn_ln_b"]


def kernel(**inputs):
    import numpy as _np
    import concourse.bacc as _bacc
    from concourse import mybir as _mybir
    from concourse.bass_utils import run_bass_kernel_spmd as _run

    nc = _bacc.Bacc("TRN2", target_bir_lowering=False, num_devices=1)
    arrays, args = {}, []
    for name in _INS:
        a = _np.ascontiguousarray(inputs[name])
        arrays[f"in_{name}_dram"] = a
        args.append(nc.dram_tensor(f"in_{name}_dram", a.shape, _mybir.dt.from_np(a.dtype), kind="ExternalInput").ap())
    shape = arrays["in_L0_attn_embeddings_dram"].shape
    args.append(nc.dram_tensor("out_0_dram", shape, _mybir.dt.float32, kind="ExternalOutput").ap())
    moe_block(nc, *args)
    r = _run(nc, [arrays], core_ids=[0])
    return r.results[0]["out_0_dram"]
```

```python
from contextlib import ExitStack

import concourse.bass as bass
from concourse import mybir

F32 = mybir.dt.float32
F16 = mybir.dt.float16
BF16 = mybir.dt.bfloat16
I32 = mybir.dt.int32
U32 = mybir.dt.uint32
U8 = mybir.dt.uint8
ALU = mybir.AluOpType
ACT = mybir.ActivationFunctionType
AX = mybir.AxisListType

P = 128
GROUPS = (4, 4)
UNROLL = 16
LAG = 2
TEMPERATURE = 0.9
EPS = 1e-5
WSCALE = 64.0
MASKED = -1e30
RSQRT_MAGIC = float(0x5F3759DF)


def moe_block(nc, emb, W_Q, W_K, W_V, gate_w, gate_b, w1, b1, w2, b2, ln_g, ln_b, out):
    B, S, D = emb.shape
    E, _, F = w1.shape
    TB = S // P
    NT = B * TB
    N = NT * P
    FC = F // P
    TOPK = 2
    SCALE = float(D) ** -0.5
    assert D == P and TB == 4 and sum(GROUPS) == B and E == 8 and GROUPS[0] == E // 2

    group_tiles, group_first, group_b0 = [], [], []
    for g, nb in enumerate(GROUPS):
        group_first.append(sum(group_tiles))
        group_b0.append(sum(GROUPS[:g]))
        group_tiles.append(nb * TB * TOPK + E - 1)
    J = sum(group_tiles)
    BODIES = -(-J // UNROLL)
    LAST = J - (BODIES - 1) * UNROLL
    JP = BODIES * UNROLL
    PREFILL = JP // B
    assert JP % B == 0
    SPLIT = group_first[1] // UNROLL
    ROW = D + 2
    GATE, BACK = D, D + 1

    slots = nc.dram_tensor("slots", [JP * P, ROW], F32, kind="Internal").ap()
    returned = nc.dram_tensor("returned", [TOPK * N + JP * P, D], F32, kind="Internal").ap()

    ctx = ExitStack()
    with ctx:
        def sb(name, shape, dt=F32):
            return ctx.enter_context(nc.sbuf_tensor(name, shape, dt))

        def sem(name):
            return ctx.enter_context(nc.semaphore(name))

        ident = sb("ident", [P, P])
        ident_h = sb("ident_h", [P, P], F16)
        ident_b = sb("ident_b", [P, P], BF16)
        mask = sb("mask", [P, P], BF16)
        before = sb("before", [P, P], F16)
        ones_h = sb("ones_h", [P, P], F16)
        ones = sb("ones", [P, 64])
        unused = sb("unused", [P, 1])
        expert_id = sb("expert_id", [P, E])
        wscale = sb("wscale", [P, 1])
        tile_start = sb("tile_start", [1, max(group_tiles)])
        wq, wk, wv = (sb(n, [P, D]) for n in ("wq", "wk", "wv"))
        wqkT = sb("wqkT", [P, 2 * D])
        mqk = sb("mqk", [P, D])
        x_in = sb("x_in", [P, TB, D])
        x_res = sb("x_res", [P, TB, D])
        xT = sb("xT", [P, S])
        gT = sb("gT", [P, S])
        v = sb("v", [P, TB, D])
        OFF = [P * i * (i + 1) // 2 for i in range(TB + 1)]
        probs = sb("probs", [P, OFF[TB]])
        probsT = sb("probsT", [P, OFF[TB]])
        negmax = sb("negmax", [P, NT])
        rowsum = sb("rowsum", [P, NT])
        rinv = sb("rinv", [P, TB])
        z = sb("z", [P, TB, D])
        stats = sb("stats", [P, TB, 6])
        moments = sb("moments", [P, TB, 2])
        rstd, shift = sb("rstd", [P, TB]), sb("shift", [P, TB])
        var, square = sb("var", [P, TB]), sb("square", [P, TB])
        xn = sb("xn", [P, TB, D])
        xnT = sb("xnT", [P, S])
        x1 = sb("x1", [P, NT, D])
        gw = sb("gw", [P, E])
        gb = sb("gb", [P, E])
        lng = sb("lng", [P, D])
        lnb = sb("lnb", [P, D])
        logits = sb("logits", [P, TB, E])
        top = sb("top", [P, TB, E])
        topi = sb("topi", [P, TB, E], U32)
        gap = sb("gap", [P, NT])
        egap = sb("egap", [P, NT])
        p1 = sb("p1", [P, NT])
        chosen = sb("chosen", [P, TOPK, NT, E], F16)
        NG = max(GROUPS) * TB * TOPK
        counts = sb("counts", [P, 2 * NG * E])
        running = sb("running", [P, 1 + NG, E])
        place = sb("place", [P, NG, E])
        padded_i = sb("padded_i", [P, E], I32)
        padded = sb("padded", [P, E])
        ends = sb("ends", [P, E])
        base = sb("base", [P, E])
        slot_f = sb("slot_f", [P, NG])
        slot_of = sb("slot_of", [P, len(GROUPS), NG], U32)
        HB = 4
        passed = sb("passed", [1, max(group_tiles), E])
        passed_n = sb("passed_n", [1, max(group_tiles)])
        expert_of = sb("expert_of", [1, LAG + J + 2], I32)
        rows = sb("rows", [P, TOPK, NT, ROW])
        W = 2 * F
        wf = sb("wf", [P, 2, W])
        PART = 2 * W + P
        experts = sb("experts", [P, E * PART], F16)
        BW, LO = F + D, 32
        bias_f = sb("bias_f", [LO + E, BW])
        bias_t = sb("bias_t", [LO + E, BW], F16)
        bias = sb("bias", [P, BW], F16)
        y_low = sb("y_low", [P, HB, D])
        slot_x = sb("slot_x", [P, HB, D])
        slot_meta = sb("slot_meta", [P, JP, 2])
        slot_xT = sb("slot_xT", [P, 2, 2 * P], F16)
        h = sb("h", [P, 2, F])
        hh, hl = sb("hh", [P, HB, F], F16), sb("hl", [P, HB, F], F16)
        y = sb("y", [P, JP, ROW])
        FULL = GROUPS[0] * TB // 2
        HALF, MOST = FULL // 2, FULL * 3 // 4
        assert GROUPS[1] == GROUPS[0]
        SETS = [(t0, t0 + FULL, t0 // (2 * FULL)) for t0 in range(0, NT, FULL)]
        TA = group_b0[1] * TB
        SUM_FROM = BODIES - 2
        assert TA == UNROLL
        pair = [rows[:, k, :, 0:D] for k in range(TOPK)]
        sum_stats = sb("sum_stats", [P, NT, 6])
        sum_moments = sb("sum_moments", [P, NT, 2])
        sum_var, sum_tmp = sb("sum_var", [P, NT]), sb("sum_tmp", [P, NT])
        sum_rstd, sum_shift = sb("sum_rstd", [P, NT]), sb("sum_shift", [P, NT])

        bank = [ctx.enter_context(nc.psum_tensor(f"bank{i}", [P, 512], F32)) for i in range(8)]
        A0, A1, S01, S2, S3, T0, T1, O = bank
        score = [S01[:, 0:P], S01[:, P:3 * P], S2[:, 0:3 * P], S3[:, 0:4 * P]]
        psT, psH, psY = (A0, A1), (S2, S3), (T0, T1, O, S01)

        def prefix_psum(g):
            return (A1, S01)[g][:, 0:2 * TOPK * GROUPS[g] * TB * E]

        const_ready = sem("const_ready")
        ones_ready = sem("ones_ready")
        w_loaded = sem("w_loaded")
        small_loaded = sem("small_loaded")
        x_in_loaded = sem("x_in_loaded")
        x_res_loaded = sem("x_res_loaded")
        ew_loaded = [sem(f"ew_loaded{k}") for k in range(2)]
        prefilled = sem("prefilled")
        wT_psum, wT_ready = sem("wT_psum"), sem("wT_ready")
        m_psum, m_ready = sem("m_psum"), sem("m_ready")
        xT_psum, xT_ready = sem("xT_psum"), sem("xT_ready")
        g_psum, g_ready = sem("g_psum"), sem("g_ready")
        v_psum, v_ready = sem("v_psum"), sem("v_ready")
        scores_psum, negmax_ready = sem("scores_psum"), sem("negmax_ready")
        probs_ready = sem("probs_ready")
        pT_psum, pT_ready = sem("pT_psum"), sem("pT_ready")
        attn_psum, attn_read = sem("attn_psum"), sem("attn_read")
        xn_ready, xnT_psum, xnT_ready = sem("xn_ready"), sem("xnT_psum"), sem("xnT_ready")
        rstd_ready, high_ready = sem("rstd_ready"), sem("high_ready")
        halves_ready, x1_kept = sem("halves_ready"), sem("x1_kept")
        rows_copied = [sem(f"rows_copied{g}") for g in range(len(GROUPS))]
        logits_psum, logits_read = sem("logits_psum"), sem("logits_read")
        chosen_ready = sem("chosen_ready")
        route_psum, route_read = sem("route_psum"), sem("route_read")
        egap_ready = sem("egap_ready")
        dispatch_ready, numbers_ready = sem("dispatch_ready"), sem("numbers_ready")
        dispatched = [sem(f"dispatched{g}") for g in range(len(GROUPS))]
        ws_ready = sem("ws_ready")
        wh_ready, wl_ready = sem("wh_ready"), sem("wl_ready")
        bias_loaded, bias_ready = sem("bias_loaded"), sem("bias_ready")
        slot_loaded = [sem(f"slot_loaded{s}") for s in range(HB)]
        meta_loaded = sem("meta_loaded")
        wait_held = sem("wait_held")
        slotT_psum, slotT_ready = sem("slotT_psum"), sem("slotT_ready")
        h_psum, gelu_ready, h_split = sem("h_psum"), sem("gelu_ready"), sem("h_split")
        y_psum, y_low_ready, y_ready = sem("y_psum"), sem("y_low_ready"), sem("y_ready")
        y_returned = [sem(f"y_returned{g}") for g in range(len(GROUPS))]
        pair_loaded = [sem(f"pair_loaded{i}") for i in range(len(SETS))]
        moments_ready = [sem(f"moments_ready{i}") for i in range(len(SETS))]
        normed = [sem(f"normed{i}") for i in range(len(SETS))]
        x1_ready, scaled, added = sem("x1_ready"), sem("scaled"), sem("added")
        summed = [sem(f"summed{i}") for i in range(len(SETS))]
        res_ready, stored = [sem(f"res_ready{i}") for i in range(len(SETS))], sem("stored")
        rest_ready = sem("rest_ready")
        pairs_added = sem("pairs_added")

        NCONST, FIRST_CONST = 14, 7
        UNITS = 3
        UNIT = [(0, 1), (2,), (3,)]
        block = ctx.enter_context(nc.Block())

        emb_t = emb.rearrange("b (t p) d -> b p t d", p=P)

        def halves_of(b):
            return rows[:].bitcast(F16)[:, 0, bass.ds(b * TB, TB), :]

        def load_pair(engine, i, t0, t1):
            for k in range(TOPK):
                engine.dma_start(pair[k][:, t0:t1, :],
                                 returned[k * N + t0 * P:k * N + t1 * P, :].rearrange("(t p) d -> p t d", p=P)).then_inc(pair_loaded[i], 16)

        def wf_chunks(k):
            return wf[:, k, :].rearrange("p (c d) -> p c d", d=P)

        def chunks(e, low):
            return experts[:, bass.ds(e * PART, 2 * W)].rearrange("p (c k d) -> p c k d", k=2, d=P)[:, :, low, :]

        @block.sync
        def _(sp):
            def batch(x, b):
                return x[b] if isinstance(b, int) else x[bass.ds(b, 1)].rearrange("a p t d -> (a p) t d")

            def prefill(b):
                sp.dma_start(slots[bass.ds(b * (PREFILL * P), PREFILL * P), :].rearrange("(j p) w -> p j w", p=P),
                             y[:, bass.ds(b * PREFILL, PREFILL), :]).then_inc(prefilled, 16)

            def keep_x1(b):
                sp.wait_ge(xn_ready, b + 1)
                sp.dma_start(x1[:, bass.ds(b * TB, TB), :], xn[:]).then_inc(x1_kept, 16)

            def copy_rows(b, group):
                tiles = bass.ds(b * TB, TB)
                sp.wait_ge(halves_ready, b + 1)
                sp.dma_start(rows[:, 1, tiles, 0:D], rows[:, 0, tiles, 0:D]).then_inc(rows_copied[group], 16)

            def load_x_in(b):
                sp.wait_ge(xT_psum, b)
                sp.dma_start(x_in[:], batch(emb_t, b)).then_inc(x_in_loaded, 16)

            def load_x_res(b):
                sp.wait_ge(attn_read, b)
                sp.dma_start(x_res[:], batch(emb_t, b)).then_inc(x_res_loaded, 16)

            def load_experts(pair):
                for k in range(2):
                    e = 2 * pair + k
                    if not isinstance(e, int) or e >= 2:
                        sp.wait_ge(wl_ready, e - 1)
                    sp.dma_start(wf[:, k, 0:F], w1[bass.ds(e, 1)].rearrange("a p f -> (a p) f")).then_inc(ew_loaded[k], 16)
                    sp.dma_start(wf[:, k, F:W].rearrange("p (c d) -> p c d", c=FC),
                                 w2[bass.ds(e, 1)].rearrange("a (c p) d -> p (a c) d", p=P)).then_inc(ew_loaded[k], 16)

            def beside_step(b, group, experts=False):
                load_x_in(b + 2)
                if experts:
                    load_experts(b)
                keep_x1(b - 1)
                prefill(b)
                load_x_res(b + 1)
                copy_rows(b - 1, group)

            sp.dma_start(x_in[:], emb_t[0]).then_inc(x_in_loaded, 16)
            sp.dma_start(wq[:], W_Q).then_inc(w_loaded, 16)
            sp.dma_start(wk[:], W_K).then_inc(w_loaded, 16)
            sp.dma_start(wv[:], W_V).then_inc(w_loaded, 16)
            sp.dma_start(x_res[:], emb_t[0]).then_inc(x_res_loaded, 16)
            load_experts(0)
            sp.dma_start(gw[:], gate_w).then_inc(small_loaded, 16)
            for row, src, n in ((gb, gate_b, E), (lng, ln_g, D), (lnb, ln_b, D)):
                sp.dma_start(row[:], src.rearrange("(a e) -> a e", a=1).broadcast_to([P, n])).then_inc(small_loaded, 16)
            for r in (0, LO):
                sp.dma_start(bias_f[r:r + E, 0:F], b1).then_inc(bias_loaded, 16)
                sp.dma_start(bias_f[r:r + E, F:BW], b2).then_inc(bias_loaded, 16)
            load_x_in(1)
            load_x_in(2)
            load_x_res(1)
            sp.wait_ge(const_ready, NCONST)
            prefill(0)
            with sp.Fori(1, E // 2) as b:
                beside_step(b, 0, experts=True)
            for b in range(E // 2, GROUPS[0] + 1):
                beside_step(b, 0)
            for b in range(GROUPS[0] + 1, B - 2):
                beside_step(b, 1)
            keep_x1(B - 3)
            prefill(B - 2)
            load_x_res(B - 1)
            copy_rows(B - 3, 1)
            prefill(B - 1)
            keep_x1(B - 2)
            copy_rows(B - 2, 1)
            keep_x1(B - 1)

            for g in range(len(GROUPS)):
                sp.wait_ge(dispatched[g], 16 * TOPK * GROUPS[g] * TB)
                i0, i1 = ((0, SPLIT), (SPLIT, BODIES))[g]

                def load_meta(i):
                    sp.dma_start(slot_meta[:, bass.ds(i * UNROLL, UNROLL), :],
                                 slots[bass.ds(i * (UNROLL * P), UNROLL * P), GATE:ROW]
                                 .rearrange("(j p) w -> p j w", p=P)).then_inc(meta_loaded, 16)

                def slot_loads(i, first=False):
                    if not first:
                        sp.wait_ge(meta_loaded, 16 * i)
                        load_meta(i)
                    first_slot = i * (UNROLL * P) if isinstance(i, int) else sp.snap(i * (UNROLL * P))
                    for s in range(UNROLL):
                        if not first:
                            sp.wait_ge(slotT_psum, i * UNROLL + (s - HB + 1))
                            sp.sem_inc(wait_held, 1)
                        elif s >= HB:
                            sp.wait_ge(slotT_psum, s - HB + 1)
                        if isinstance(i, int) and i == SUM_FROM and s == LAG:
                            sp.wait_ge(y_returned[0], 16 * group_tiles[0])
                            for n, (t0, t1, _) in enumerate(SETS[0:2]):
                                load_pair(sp, n, t0, t1)
                        sp.dma_start(slot_x[:, s % HB, :], slots[bass.ds(first_slot + s * P, P), 0:D]).then_inc(slot_loaded[s % HB], 16)
                        if first and s == 1:
                            load_meta(0)
                            copy_rows(B - 1, 1)

                if i0 == 0:
                    slot_loads(0, first=True)
                    i0 = 1
                with sp.Fori(i0, min(i1, SUM_FROM)) as i:
                    slot_loads(i)
                for i in range(SUM_FROM, i1):
                    slot_loads(i)

            sp.wait_ge(y_returned[1], 16 * group_tiles[1])
            for i, (t0, t1, g) in enumerate(SETS):
                if g == 1:
                    load_pair(sp, i, t0, t1)
            out_p = out.rearrange("b (t p) d -> p (b t) d", p=P)
            stores = [(0, 1, 0, FULL), (1, 1, 0, FULL),
                      (3, 1, 0, HALF), (2, 1, 0, HALF), (3, 2, HALF, FULL), (2, 2, HALF, FULL)]
            for n, (i, count, first, end) in enumerate(stores):
                t0 = SETS[i][0]
                if n == len(stores) - 1:
                    sp.wait_ge(rest_ready, 1)
                sp.wait_ge(res_ready[i], count)
                sp.dma_start(out_p[:, t0 + first:t0 + end, :], pair[1][:, t0 + first:t0 + end, :]).then_inc(stored, 16)
            sp.wait_ge(stored, 16 * len(stores))

        @block.tensor
        def _(pe):
            def transpose_x(b):
                pe.wait_ge(x_in_loaded, (b + 1) * 16)
                if not isinstance(b, int) or b:
                    pe.wait_ge(v_ready, b)
                for t in range(TB):
                    m = nc.tensor.transpose(A0[:, t * P:(t + 1) * P], x_in[:, t, :], ident[:])
                m.then_inc(xT_psum, 1)

            def project_g(b):
                pe.wait_ge(xT_ready, b + 1)
                nc.tensor.matmul(A0[:], mqk[:], xT[:], start=True, stop=True).then_inc(g_psum, 1)

            def project_v(b):
                pe.wait_ge(g_ready, b + 1)
                for t in range(TB):
                    m = nc.tensor.matmul(A0[:, t * P:(t + 1) * P], xT[:, t * P:(t + 1) * P], wv[:], start=True, stop=True)
                m.then_inc(v_psum, 1)

            def scores(b):
                pe.wait_ge(g_ready, b + 1)
                if not isinstance(b, int) or b:
                    pe.wait_ge(probs_ready, b * UNITS)
                for u in range(UNITS):
                    for i in UNIT[u]:
                        nc.tensor.matmul(score[i], gT[:, i * P:(i + 1) * P], xT[:, 0:(i + 1) * P], start=True, stop=False)
                        m = nc.tensor.matmul(score[i][:, i * P:(i + 1) * P], ident_b[:], mask[:], start=False, stop=True)
                    m.then_inc(scores_psum, 1)

            def transpose_probs(b, u):
                bk = (T0, T1, T0)[u]
                pe.wait_ge(probs_ready, b * UNITS + (u + 1))
                if u == 2:
                    pe.wait_ge(pT_ready, b * UNITS + 1)
                elif u == 0 and (not isinstance(b, int) or b):
                    pe.wait_ge(pT_ready, b * UNITS)
                o0 = OFF[UNIT[u][0]]
                for i in UNIT[u]:
                    for j in range(i + 1):
                        o = OFF[i] + j * P
                        m = nc.tensor.transpose(bk[:, o - o0:o - o0 + P], probs[:, o:o + P], ident[:])
                m.then_inc(pT_psum, 1)

            def weigh_values(b, u):
                pe.wait_ge(pT_ready, b * UNITS + (u + 1))
                if u == 0:
                    pe.wait_ge(v_ready, b + 1)
                    if not isinstance(b, int) or b:
                        pe.wait_ge(attn_read, b)
                for i in UNIT[u]:
                    for j in range(i + 1):
                        o = OFF[i] + j * P
                        m = nc.tensor.matmul(O[:, i * P:(i + 1) * P], probsT[:, o:o + P], v[:, j, :],
                                             start=(j == 0), stop=(j == i))
                if u == UNITS - 1:
                    m.then_inc(attn_psum, 1)

            def transpose_xn(b):
                pe.wait_ge(xn_ready, b + 1)
                if not isinstance(b, int) or b:
                    pe.wait_ge(logits_read, b)
                for t in range(TB):
                    m = nc.tensor.transpose(A1[:, t * P:(t + 1) * P], xn[:, t, :], ident[:])
                m.then_inc(xnT_psum, 1)

            def gate(b):
                pe.wait_ge(xnT_ready, b + 1)
                for t in range(TB):
                    m = nc.tensor.matmul(A1[:, t * E:(t + 1) * E], xnT[:, t * P:(t + 1) * P], gw[:], start=True, stop=True)
                m.then_inc(logits_psum, 1)

            def step(b, first=False, last=False, routes=False):
                if not last:
                    transpose_x(b + 1)
                transpose_probs(b, 0)
                transpose_probs(b, 1)
                if not last:
                    project_g(b + 1)
                if routes:
                    pe.wait_ge(logits_read, b - 1)
                    prefix_sums(0)
                weigh_values(b, 0)
                transpose_probs(b, 2)
                weigh_values(b, 1)
                weigh_values(b, 2)
                if not last:
                    project_v(b + 1)
                if routes:
                    pe.wait_ge(route_read, 1)
                if not first:
                    transpose_xn(b - 1)
                if not last:
                    scores(b + 1)
                if not first:
                    gate(b - 1)

            def prefix_sums(g):
                pe.wait_ge(chosen_ready, group_b0[g] + GROUPS[g])
                t0, n = group_b0[g] * TB, GROUPS[g] * TB
                picked = chosen[:, :, t0:t0 + n, :].rearrange("p k t e -> p k (t e)")
                for k, weights in enumerate((before, ones_h)):
                    where = prefix_psum(g).rearrange("p (i k c) -> p i k c", i=2, k=TOPK)[:, k, :, :]
                    m = nc.tensor.matmul(where, weights[:], picked, start=True, stop=True)
                m.then_inc(route_psum, 1)

            pe.wait_ge(const_ready, FIRST_CONST)
            pe.wait_ge(w_loaded, 48)
            nc.tensor.transpose(A1[:, 0:P], wq[:], ident[:])
            nc.tensor.transpose(A1[:, P:2 * P], wk[:], ident[:]).then_inc(wT_psum, 1)
            transpose_x(0)
            pe.wait_ge(wT_ready, 1)
            nc.tensor.matmul(A1[:, 2 * P:3 * P], wqkT[:, 0:P], wqkT[:, P:2 * P], start=True, stop=True).then_inc(m_psum, 1)
            pe.wait_ge(m_ready, 1)
            pe.wait_ge(small_loaded, 64)
            project_g(0)
            project_v(0)
            scores(0)

            ROUTE_AT = group_b0[1] + 1
            step(0, first=True)
            with pe.Fori(1, ROUTE_AT) as b:
                step(b)
            step(ROUTE_AT, routes=True)
            with pe.Fori(ROUTE_AT + 1, B - 1) as b:
                step(b)
            step(B - 1, last=True)
            transpose_xn(B - 1)
            gate(B - 1)

            pe.wait_ge(wl_ready, E)
            pe.wait_ge(wh_ready, E)
            pe.wait_ge(bias_ready, 5)
            pe.wait_ge(numbers_ready, 1)
            pe.wait_ge(v_ready, B)
            pe.wait_ge(logits_read, B)

            def transpose_slots(i, s):
                pe.wait_ge(slot_loaded[s % HB], i * (UNROLL // HB * 16) + (s // HB + 1) * 16)
                src = slot_x[:, s % HB, :].bitcast(F16)
                dst = psT[s % 2][:, 0:P].bitcast(F16)
                for k in range(2):
                    m = nc.tensor.transpose(dst[:, k * P:(k + 1) * P], src[:, k * D:(k + 1) * D], ident_h[:])
                m.then_inc(slotT_psum, 1)

            def of_expert(col, n, offset):
                return experts[:].bitcast(U8)[:, 2 * col:][:, bass.ds(offset, 2 * n)].bitcast(F16)

            def expand(i, s, e):
                pe.wait_ge(slotT_ready, i * UNROLL + (s + 1))
                xh, xl = slot_xT[:, s % 2, 0:P], slot_xT[:, s % 2, P:2 * P]
                picked = of_expert(2 * W, P, e)
                for c in range(FC):
                    o = psH[s % 2][:, c * P:(c + 1) * P]
                    high, low = of_expert(2 * c * P, P, e), of_expert((2 * c + 1) * P, P, e)
                    nc.tensor.matmul(o, high, xh, start=True, stop=False)
                    nc.tensor.matmul(o, high, xl, start=False, stop=False)
                    nc.tensor.matmul(o, low, xh, start=False, stop=False)
                    m = nc.tensor.matmul(o, bias[:, c * P:(c + 1) * P], picked, start=False, stop=True)
                m.then_inc(h_psum, 1)

            def contract(j, s, e):
                pe.wait_ge(h_split, j + 1)
                both, main = psY[s % HB][:, 0:2 * D], psY[s % HB][:, 0:D]
                for c in range(FC):
                    col, rows_c = 2 * (F + c * D), slice(c * P, (c + 1) * P)
                    if c == FC - 1:
                        nc.tensor.matmul(main, of_expert(2 * W, P, e), bias[:, F:BW], start=False, stop=False)
                        nc.tensor.matmul(main, hl[:, s % HB, rows_c], of_expert(col, D, e), start=False, stop=False)
                    m = nc.tensor.matmul(both, hh[:, s % HB, rows_c], of_expert(col, 2 * D, e), start=(c == 0), stop=(c == FC - 1))
                    if c < FC - 1:
                        nc.tensor.matmul(main, hl[:, s % HB, rows_c], of_expert(col, D, e), start=False, stop=False)
                m.then_inc(y_psum, 1)

            def expert_numbers(first, n):
                _, e = nc.values_load_multi_w_load_instructions(expert_of[0:1, bass.ds(first, n)],
                                                                engines=[mybir.EngineType.PE], min_val=0, max_val=E - 1,
                                                                skip_runtime_bounds_check_because="assign_link() computes 0 .. E - 1")
                return [pe.snap(x * (2 * PART)) for x in e]

            def body(i, first=False, last=False):
                e = expert_numbers(i * UNROLL, UNROLL + LAG)
                tiles = LAST if last else UNROLL
                for s in range(tiles):
                    if s < tiles - 1:
                        transpose_slots(i, s + 1)
                    elif not last:
                        transpose_slots(i + 1, 0)
                    if first and s == LAG + 2:
                        pe.wait_ge(attn_read, B)
                    if first and s == LAG + 3:
                        pe.wait_ge(route_read, 2)
                    if not first or s >= LAG:
                        contract(i * UNROLL + s - LAG, (s - LAG) % UNROLL, e[s])
                    expand(i, s, e[s + LAG])
                    if first and s == 0:
                        prefix_sums(1)

            transpose_slots(0, 0)
            body(0, first=True)
            with pe.Fori(1, SPLIT) as i:
                body(i)
            pe.wait_ge(numbers_ready, 2)
            with pe.Fori(SPLIT, BODIES - 1) as i:
                body(i)
            body(BODIES - 1, last=True)
            e = expert_numbers(J, LAG)
            for s in range(LAG):
                contract(J - LAG + s, (J - LAG + s) % UNROLL, e[s])

        @block.scalar
        def _(act):
            def copy_g(b):
                act.wait_ge(g_psum, b + 1)
                nc.scalar.activation(gT[:], A0[:], ACT.Copy).then_inc(g_ready, 1)

            def copy_v(b):
                act.wait_ge(v_psum, b + 1)
                nc.scalar.activation(v[:].rearrange("p t d -> p (t d)"), A0[:], ACT.Copy).then_inc(v_ready, 1)

            def copy_xnT(b):
                act.wait_ge(xnT_psum, b + 1)
                nc.scalar.activation(xnT[:], A1[:], ACT.Copy).then_inc(xnT_ready, 1)

            def copy_probsT(b, u):
                act.wait_ge(pT_psum, b * UNITS + (u + 1))
                a, n = OFF[UNIT[u][0]], OFF[UNIT[u][-1] + 1] - OFF[UNIT[u][0]]
                nc.scalar.activation(probsT[:, a:a + n], (T0, T1, T0)[u][:, 0:n], ACT.Copy).then_inc(pT_ready, 1)

            def normalise_x(b, first=False):
                act.wait_ge(rstd_ready, b + 1)
                if not first:
                    act.wait_ge(x1_kept, b * 16)
                    act.wait_ge(halves_ready, b)
                for t in range(TB):
                    m = nc.scalar.activation(xn[:, t, :], z[:, t, :], ACT.Identity, bias=shift[:, t:t + 1], scale=rstd[:, t:t + 1])
                m.then_inc(xn_ready, 1)
                act.wait_ge(xn_ready, b + 1)
                nc.scalar.activation(halves_of(b)[:, :, 0:D], xn[:], ACT.Copy).then_inc(high_ready, 1)

            def exponentials(b):
                for u in range(UNITS):
                    act.wait_ge(negmax_ready, b * UNITS + (u + 1))
                    for i in UNIT[u]:
                        col = bass.ds(b * TB + i, 1)
                        m = nc.scalar.activation(probs[:, OFF[i]:OFF[i + 1]], score[i], ACT.Exp,
                                                 bias=negmax[:, col], accum_out=rowsum[:, col])
                    m.then_inc(probs_ready, 1)

            def copy_xT(b):
                act.wait_ge(xT_psum, b + 1)
                nc.scalar.activation(xT[:], A0[:], ACT.Copy).then_inc(xT_ready, 1)

            def weights_high(e, k):
                act.wait_ge(ws_ready, e + 1)
                nc.scalar.activation(chunks(e, 0), wf_chunks(k), ACT.Copy).then_inc(wh_ready, 1)

            def step(b, first=False, last=False, pair=None, routes=False):
                if not last:
                    copy_xT(b + 1)
                copy_probsT(b, 0)
                copy_probsT(b, 1)
                if not last:
                    copy_g(b + 1)
                if pair is not None:
                    weights_high(2 * pair, 0)
                    weights_high(2 * pair + 1, 1)
                if routes:
                    gate_exp(0)
                copy_probsT(b, 2)
                if not first:
                    normalise_x(b - 1, first=isinstance(b, int) and b == 1)
                if not last:
                    copy_v(b + 1)
                if not first:
                    copy_xnT(b - 1)
                if not last:
                    exponentials(b + 1)

            def gate_exp(g):
                t0, n = group_b0[g] * TB, GROUPS[g] * TB
                act.wait_ge(chosen_ready, group_b0[g] + GROUPS[g])
                nc.scalar.activation(egap[:, t0:t0 + n], gap[:, t0:t0 + n], ACT.Exp,
                                     scale=1.0 / TEMPERATURE).then_inc(egap_ready, 1)

            act.wait_ge(ones_ready, 1)
            nc.scalar.activation(egap[:, 0:1], ones[:, 0:1], ACT.Exp)
            act.wait_ge(wT_psum, 1)
            nc.scalar.activation(wqkT[:], A1[:, 0:2 * P], ACT.Copy).then_inc(wT_ready, 1)
            act.wait_ge(m_psum, 1)
            nc.scalar.activation(mqk[:], A1[:, 2 * P:3 * P], ACT.Copy, scale=SCALE).then_inc(m_ready, 1)
            copy_xT(0)
            copy_g(0)
            copy_v(0)
            exponentials(0)
            step(0, first=True)
            ROUTE_AT = group_b0[1] + 1
            step(1, pair=0)
            with act.Fori(2, E // 2 + 1) as b:
                step(b, pair=b - 1)
            step(ROUTE_AT, routes=True)
            with act.Fori(ROUTE_AT + 1, B - 1) as b:
                step(b)
            step(B - 1, last=True)
            normalise_x(B - 1)
            copy_xnT(B - 1)

            def normalise(i, second, first=0, end=FULL):
                t0 = SETS[i][0]
                act.wait_ge(moments_ready[i], second + 1)
                for t in range(t0 + first, t0 + end):
                    m = nc.scalar.activation(pair[second][:, t, :], pair[0][:, t, :], ACT.Identity,
                                             bias=sum_shift[:, t:t + 1], scale=sum_rstd[:, t:t + 1])
                m.then_inc(res_ready[i] if second else normed[i], 1)

            def copy_slots(j, s):
                act.wait_ge(slotT_psum, j + 1)
                nc.scalar.activation(slot_xT[:, s % 2, :], psT[s % 2][:, 0:P].bitcast(F16), ACT.Copy).then_inc(slotT_ready, 1)

            def gelu(j, s):
                act.wait_ge(h_psum, j + 1)
                nc.scalar.activation(h[:, s % 2, :], psH[s % 2][:], ACT.Gelu, scale=1.0 / WSCALE).then_inc(gelu_ready, 1)

            def weigh_low(j, s):
                nc.scalar.activation(y_low[:, s % HB, :], psY[s % HB][:, D:2 * D], ACT.Copy,
                                     scale=slot_meta[:, bass.ds(j, 1), 0:1].rearrange("p a d -> p (a d)")).then_inc(y_low_ready, 1)

            def body(i, first=False, last=False):
                act.wait_ge(meta_loaded, (i + 1) * 16)
                tiles = LAST if last else UNROLL
                for s in range(tiles):
                    if s < tiles - 1 or not last:
                        copy_slots(i * UNROLL + (s + 1), s + 1)
                    gelu(i * UNROLL + s, s)
                    if not first or s >= LAG:
                        weigh_low(i * UNROLL + (s - LAG), (s - LAG) % UNROLL)
                    if last and s >= LAST - 2:
                        q = HALF // 2 * (s - LAST + 2)
                        normalise(0, 0, q, q + HALF // 2)

            copy_slots(0, 0)
            gate_exp(1)
            nc.scalar.activation(unused[:], ones[:, 0:1], ACT.Gelu)
            body(0, first=True)
            with act.Fori(1, BODIES - 1) as i:
                body(i)
            body(BODIES - 1, last=True)
            for s in range(LAG):
                act.wait_ge(y_psum, J - LAG + s + 1)
                weigh_low(J - LAG + s, (J - LAG + s) % UNROLL)

            normalise(0, 0, HALF, MOST)
            normalise(1, 0)
            normalise(0, 1)
            normalise(2, 0)
            normalise(3, 0, 0, HALF)
            normalise(1, 1)
            normalise(2, 1, 0, HALF)
            normalise(2, 1, HALF, MOST)

        @block.vector
        def _(dve):
            def maxima(b):
                for u in range(UNITS):
                    dve.wait_ge(scores_psum, b * UNITS + (u + 1))
                    for i in UNIT[u]:
                        m = nc.vector.reduce_max(negmax[:, bass.ds(b * TB + i, 1)], score[i], AX.X, negate=True)
                    m.then_inc(negmax_ready, 1)

            def residual(b):
                dve.wait_ge(attn_psum, b + 1)
                nc.vector.reciprocal(rinv[:], rowsum[:, bass.ds(b * TB, TB)])
                dve.drain()
                dve.wait_ge(x_res_loaded, (b + 1) * 16)
                if not isinstance(b, int) or b:
                    dve.wait_ge(xn_ready, b)
                for t in range(TB):
                    m = nc.vector.scalar_tensor_tensor(out=z[:, t, :], in0=O[:, t * P:(t + 1) * P], scalar=rinv[:, t:t + 1],
                                                       in1=x_res[:, t, :], op0=ALU.mult, op1=ALU.add)
                m.then_inc(attn_read, 1)

            def rsqrt_step(i, r, variance, tmp):
                v = nc.vector
                if i == 0:
                    v.tensor_scalar(r.bitcast(I32), variance.bitcast(I32), -0.5, RSQRT_MAGIC, ALU.mult, ALU.add)
                elif i in (1, 5):
                    v.tensor_tensor(tmp, r, r, ALU.mult)
                elif i == 2:
                    v.tensor_tensor(tmp, tmp, variance, ALU.mult)
                elif i == 3:
                    v.scalar_tensor_tensor(out=tmp, in0=tmp, scalar=-10.0 / 3.0, in1=tmp, op0=ALU.add, op1=ALU.mult)
                elif i == 4:
                    v.scalar_tensor_tensor(out=r, in0=tmp, scalar=5.0, in1=r, op0=ALU.add, op1=ALU.mult)
                elif i == 6:
                    v.scalar_tensor_tensor(out=tmp, in0=tmp, scalar=-0.5 * 0.375 ** 3, in1=variance, op0=ALU.mult, op1=ALU.mult)
                else:
                    v.scalar_tensor_tensor(out=r, in0=tmp, scalar=1.5 * 0.375, in1=r, op0=ALU.add, op1=ALU.mult)

            def norm_and_choose(b, norm=True, choose=True):
                v = nc.vector
                c = b - 1
                ctiles = bass.ds(c * TB, TB)
                if norm:
                    dve.wait_ge(attn_read, b + 1)
                    for t in range(TB):
                        v.bn_stats(stats[:, t, :], z[:, t, :])
                if choose:
                    dve.wait_ge(logits_psum, b)
                    v.tensor_tensor(logits[:], A1[:, 0:TB * E].rearrange("p (t e) -> p t e", t=TB),
                                    gb[:].rearrange("p (a e) -> p a e", a=1).broadcast_to([P, TB, E]), ALU.add).then_inc(logits_read, 1)
                dve.drain()
                if norm:
                    for t in range(TB):
                        v.bn_aggr(moments[:, t, :], stats[:, t, :])
                if choose:
                    for t in range(TB):
                        v.max(top[:, t, :], logits[:, t, :])
                dve.drain()
                if norm:
                    v.tensor_scalar(var[:].rearrange("p (t a) -> p t a", a=1), moments[:, :, 1:2], EPS, None, ALU.add)
                if choose:
                    for t in range(TB):
                        v.max_index(topi[:, t, :], top[:, t, :], logits[:, t, :])
                    v.tensor_tensor(gap[:, ctiles].rearrange("p (t a) -> p t a", a=1), top[:, :, 1:2], top[:, :, 0:1], ALU.subtract)
                dve.drain()
                if norm:
                    rsqrt_step(0, rstd[:], var[:], square[:])
                if choose:
                    for k in range(TOPK):
                        m = v.tensor_tensor(chosen[:, k, ctiles, :],
                                            expert_id[:].rearrange("p (a e) -> p a e", a=1).broadcast_to([P, TB, E]),
                                            topi[:, :, k:k + 1].broadcast_to([P, TB, E]), ALU.is_equal)
                    m.then_inc(chosen_ready, 1)
                if norm:
                    for i in range(1, 8):
                        dve.drain()
                        rsqrt_step(i, rstd[:], var[:], square[:])
                    dve.drain()
                    v.scalar_tensor_tensor(out=shift[:].rearrange("p (t a) -> p t a", a=1), in0=moments[:, :, 0:1], scalar=-1.0,
                                           in1=rstd[:].rearrange("p (t a) -> p t a", a=1), op0=ALU.mult, op1=ALU.mult).then_inc(rstd_ready, 1)

            def low_halves(b):
                dve.wait_ge(high_ready, b + 1)
                x_high, x_low = halves_of(b)[:, :, 0:D], halves_of(b)[:, :, D:2 * D]
                nc.vector.tensor_tensor(x_low, xn[:], x_high, ALU.subtract).then_inc(halves_ready, 1)

            def step(b, first=False, last=False):
                residual(b)
                if not last:
                    maxima(b + 1)
                if not first:
                    low_halves(b - 1)
                norm_and_choose(b, choose=not first)

            def split_biases():
                dve.wait_ge(bias_loaded, 64)
                v, low = nc.vector, slice(LO, LO + E)
                v.tensor_scalar(bias_f[low, :], bias_f[low, :], WSCALE, None, ALU.mult).then_inc(bias_ready, 1)
                v.tensor_scalar(bias[0:E, :], bias_f[0:E, :], WSCALE, None, ALU.mult).then_inc(bias_ready, 1)
                dve.wait_ge(bias_ready, 2)
                v.tensor_copy(bias_t[low, :], bias_f[low, :]).then_inc(bias_ready, 1)
                dve.wait_ge(bias_ready, 3)
                v.tensor_tensor(bias[low, :], bias_f[low, :], bias_t[low, :], ALU.subtract).then_inc(bias_ready, 2)

            ROUTE_LINKS = 14

            def assign_link(g, q):
                v = nc.vector
                t0, n, nt, j0 = group_b0[g] * TB, GROUPS[g] * TB, group_tiles[g], LAG + group_first[g]
                m, w = TOPK * n, TOPK * n * E
                by_row = "p (a e) -> p a e"
                place_, gate_p, q_ = place[:, 0:m, :], p1[:, t0:t0 + n], egap[:, t0:t0 + n]
                if q == 0:
                    dve.wait_ge(route_psum, g + 1)
                    v.tensor_copy(counts[:, 0:2 * w], prefix_psum(g)).then_inc(route_read, 1)
                elif q == 1:
                    total = counts[:, w:2 * w].rearrange("p (m e) -> p m e", e=E)
                    for e in range(E):
                        v.tensor_tensor_scan(running[:, 1:1 + m, e], ones[:, 0:m], total[:, :, e], 0.0, ALU.mult, ALU.add)
                elif q == 2:
                    v.tensor_tensor(place_, counts[:, 0:w].rearrange("p (m e) -> p m e", e=E), running[:, 0:m, :], ALU.add)
                    v.tensor_scalar(padded_i[:], running[:, m, :], float(P - 1), None, ALU.add)
                elif q == 3:
                    v.tensor_scalar(padded_i[:], padded_i[:], -P, None, ALU.bitwise_and)
                elif q == 4:
                    v.tensor_copy(padded[:], padded_i[:])
                elif q == 5:
                    v.tensor_tensor_scan(ends[:], ones[:, 0:E], padded[:], 0.0, ALU.mult, ALU.add)
                elif q == 6:
                    v.tensor_tensor(base[:], ends[:], padded[:], ALU.subtract)
                elif q == 7:
                    v.tensor_tensor(place_, place_, base[:].rearrange(by_row, a=1).broadcast_to([P, m, E]), ALU.add)
                elif q == 8:
                    for k in range(TOPK):
                        place_k = place[:, k * n:(k + 1) * n, :]
                        v.tensor_tensor(place_k, place_k, chosen[:, k, t0:t0 + n, :], ALU.mult)
                    dve.wait_ge(egap_ready, g + 1)
                    v.tensor_scalar(gate_p, q_, WSCALE, WSCALE, ALU.mult, ALU.add)
                elif q == 9:
                    v.reciprocal(gate_p, gate_p)
                    v.tensor_reduce(slot_f[:, 0:m], place_, AX.X, ALU.add)
                elif q == 10:
                    v.tensor_copy(rows[:, 0, t0:t0 + n, GATE], gate_p)
                    v.tensor_tensor(rows[:, 1, t0:t0 + n, GATE], gate_p, q_, ALU.mult)
                    v.tensor_scalar(slot_of[:, g, 0:m], slot_f[:, 0:m], float(group_first[g] * P), None,
                                    ALU.add).then_inc(dispatch_ready, 1)
                elif q == 11:
                    v.tensor_tensor(passed[:, 0:nt, :],
                                    tile_start[:, 0:nt].rearrange("p (t a) -> p t a", a=1).broadcast_to([1, nt, E]),
                                    ends[0:1, :].rearrange(by_row, a=1).broadcast_to([1, nt, E]), ALU.is_ge)
                elif q == 12:
                    v.tensor_reduce(passed_n[:, 0:nt], passed[:, 0:nt, :], AX.X, ALU.add)
                else:
                    v.tensor_scalar(expert_of[:, j0:j0 + nt], passed_n[:, 0:nt], float(E - 1), None, ALU.min).then_inc(numbers_ready, 1)

            nc.vector.memset(running[:, 0, :], 0.0)
            nc.vector.memset(ones[:], 1.0).then_inc(ones_ready, 1)
            dve.wait_ge(ones_ready, 1)
            maxima(0)
            ROUTE_AT = group_b0[1] + 1
            dve.wait_ge(small_loaded, 64)
            dve.wait_ge(const_ready, NCONST)
            split_biases()
            step(0, first=True)
            with dve.Fori(1, ROUTE_AT) as b:
                step(b)
            for q in range(ROUTE_LINKS):
                assign_link(0, q)
                dve.drain()
            with dve.Fori(ROUTE_AT, B - 1) as b:
                step(b)
            step(B - 1, last=True)

            low_halves(B - 1)
            norm_and_choose(B, norm=False)
            assign_link(1, 0)
            dve.drain()

            def split(i, s, sums=(), before=(), chain=None, route=None):
                dve.wait_ge(gelu_ready, i * UNROLL + (s + 1))
                nc.vector.tensor_copy(hh[:, s % HB, :], h[:, s % 2, :])
                if chain is not None and chain < LINKS:
                    moments_link(chain, 0, TA)
                if route is not None:
                    assign_link(1, route)
                dve.drain()
                nc.vector.tensor_tensor(hl[:, s % HB, :], h[:, s % 2, :], hh[:, s % HB, :], ALU.subtract).then_inc(h_split, 1)
                for t in before:
                    nc.vector.bn_aggr(sum_moments[:, t, :], sum_stats[:, t, :])
                for t in sums:
                    dve.wait_ge(pairs_added, t // 2 + 1)
                    nc.vector.bn_stats(sum_stats[:, t, :], pair[0][:, t, :])

            def weigh(j, s):
                tile = bass.ds(j, 1)
                flat = "p a d -> p (a d)"
                dve.wait_ge(y_low_ready, j + 1)
                nc.vector.scalar_tensor_tensor(out=y[:, tile, 0:D].rearrange(flat), in0=psY[s % HB][:, 0:D],
                                               scalar=slot_meta[:, tile, 0:1].rearrange(flat), in1=y_low[:, s % HB, :],
                                               op0=ALU.mult, op1=ALU.add).then_inc(y_ready, 1)

            def tiles_of(s):
                done = max(s - LAG, 0) + max(s - UNROLL + LAG, 0)
                return range(done, done + (s >= LAG) + (s >= UNROLL - LAG))

            def body(i, first=False, last=False, sums=False):
                dve.wait_ge(meta_loaded, (i + 1) * 16)
                for s in range(LAST if last else UNROLL):
                    if sums:
                        split(i, s, tiles_of(s), tiles_of(s - 1))
                    elif last:
                        split(i, s, before=tiles_of(UNROLL - 1) if s == 0 else (), chain=s if s > 1 else None)
                    else:
                        split(i, s, route=2 * s + 1 if first and 2 * s + 1 < ROUTE_LINKS else None)
                    if not first or s >= LAG:
                        weigh(i * UNROLL + (s - LAG), (s - LAG) % UNROLL)
                    if first and 2 * s + 2 < ROUTE_LINKS:
                        assign_link(1, 2 * s + 2)
                        dve.drain()

            LINKS = 12

            def moments_link(q, t0, t1):
                rstd_, var_, tmp_ = sum_rstd[:, t0:t1], sum_var[:, t0:t1], sum_tmp[:, t0:t1]
                one = "p (t a) -> p t a"
                if q < 2:
                    half = (t0 + t1) // 2
                    for t in (range(t0, half), range(half, t1))[q]:
                        nc.vector.bn_aggr(sum_moments[:, t, :], sum_stats[:, t, :])
                elif q == 2:
                    nc.vector.tensor_scalar(var_.rearrange(one, a=1), sum_moments[:, t0:t1, 1:2], EPS, None, ALU.add)
                elif q < LINKS - 1:
                    rsqrt_step(q - 3, rstd_, var_, tmp_)
                else:
                    for i, (u0, u1, g) in enumerate(SETS):
                        if t0 <= u0 and u1 <= t1:
                            nc.vector.scalar_tensor_tensor(out=sum_shift[:, u0:u1].rearrange(one, a=1), in0=sum_moments[:, u0:u1, 0:1],
                                                           scalar=-1.0, in1=sum_rstd[:, u0:u1].rearrange(one, a=1),
                                                           op0=ALU.mult, op1=ALU.mult).then_inc(moments_ready[i], 1)

            body(0, first=True)
            with dve.Fori(1, SUM_FROM) as i:
                body(i)
            body(SUM_FROM, sums=True)
            body(BODIES - 1, last=True)
            for s in range(LAG):
                weigh(J - LAG + s, (J - LAG + s) % UNROLL)

            def moments_of(t0, t1):
                for t in range(t0, t1):
                    nc.vector.bn_stats(sum_stats[:, t, :], pair[0][:, t, :])
                for q in range(LINKS):
                    if q != 1:
                        dve.drain()
                    moments_link(q, t0, t1)

            def normalise(i, second, first, end):
                t0 = SETS[i][0]
                for t in range(t0 + first, t0 + end):
                    m = nc.vector.tensor_scalar(pair[second][:, t, :], pair[0][:, t, :], sum_moments[:, t, 0:1],
                                                sum_rstd[:, t:t + 1], ALU.subtract, ALU.mult)
                return m

            def times_ln_g(i, first, end):
                t0 = SETS[i][0]
                z_ = pair[0][:, t0 + first:t0 + end, :]
                nc.vector.tensor_tensor(z_, z_, lng[:].rearrange("p (a d) -> p a d", a=1).broadcast_to([P, end - first, D]), ALU.mult)

            def plus_residual(i, first, end):
                t0 = SETS[i][0]
                z_ = pair[0][:, t0 + first:t0 + end, :]
                nc.vector.tensor_tensor(z_, z_, x1[:, t0 + first:t0 + end, :], ALU.add)

            first_, a1, b0, b1 = SETS
            normalise(0, 0, MOST, FULL)
            dve.drain()
            dve.wait_ge(normed[0], 3)
            dve.wait_ge(x1_ready, 1)
            times_ln_g(0, 0, FULL)
            dve.drain()
            plus_residual(0, 0, FULL)
            dve.drain()
            moments_of(first_[0], first_[1])
            dve.wait_ge(pair_loaded[2], 16 * TOPK)
            nc.vector.tensor_tensor(pair[0][:, b0[0]:b0[1], :], pair[0][:, b0[0]:b0[1], :], pair[1][:, b0[0]:b0[1], :], ALU.add)
            dve.drain()
            dve.wait_ge(summed[1], 1)
            moments_of(a1[0], b0[1])
            dve.wait_ge(added, 1)
            moments_of(b1[0], b1[1])
            dve.drain()
            normalise(3, 0, HALF, FULL)
            dve.drain()
            times_ln_g(3, HALF, FULL)
            dve.wait_ge(normed[3], 1)
            times_ln_g(3, 0, HALF)
            dve.drain()
            plus_residual(3, 0, FULL)
            dve.drain()
            dve.wait_ge(summed[2], 1)
            moments_of(b0[0], b1[1])
            dve.drain()
            normalise(3, 1, 0, HALF).then_inc(res_ready[3], 1)
            normalise(3, 1, HALF, FULL).then_inc(res_ready[3], 1)
            normalise(2, 1, MOST, FULL).then_inc(rest_ready, 1)

        @block.gpsimd
        def _(pool):
            made = sem("made")
            g = nc.gpsimd
            g.memset(ident[:], 0.0).then_inc(made, 1)
            g.memset(wscale[:], WSCALE).then_inc(const_ready, 1)
            g.memset(mask[:], 0.0).then_inc(made, 1)
            g.memset(before[:], 1.0).then_inc(made, 1)
            g.memset(ones_h[:], 1.0).then_inc(const_ready, 1)
            pool.wait_ge(made, 3)
            g.affine_select(out=ident[:], in_=ident[:], compare_op=ALU.not_equal, fill=1.0, base=0,
                            pattern=[[-1, P]], channel_multiplier=1).then_inc(const_ready, 1)
            g.affine_select(out=mask[:], in_=mask[:], compare_op=ALU.is_ge, fill=MASKED, base=0,
                            pattern=[[-1, P]], channel_multiplier=1).then_inc(const_ready, 1)
            g.affine_select(out=before[:], in_=before[:], compare_op=ALU.is_gt, fill=0.0, base=0,
                            pattern=[[1, P]], channel_multiplier=-1).then_inc(const_ready, 1)
            pool.wait_ge(const_ready, 5)
            g.tensor_copy(ident_h[:], ident[:]).then_inc(const_ready, 1)
            g.tensor_copy(ident_b[:], ident[:]).then_inc(const_ready, 1)
            g.iota(expert_id[:], [[1, E]], base=0, channel_multiplier=0, allow_small_or_imprecise_dtypes=True).then_inc(const_ready, 1)
            g.iota(tile_start[:], [[P, max(group_tiles)]], base=0, channel_multiplier=0,
                   allow_small_or_imprecise_dtypes=True).then_inc(const_ready, 1)
            g.iota(rows[:, :, :, BACK].bitcast(I32), [[N, TOPK], [P, NT]], base=0, channel_multiplier=1).then_inc(const_ready, 1)
            g.memset(y[:], 0.0).then_inc(made, 1)
            pool.wait_ge(made, 4)
            g.iota(y[:, :, BACK].bitcast(I32), [[P, JP]], base=TOPK * N, channel_multiplier=1).then_inc(const_ready, 1)
            g.memset(expert_of[:], 0).then_inc(const_ready, 1)
            g.memset(bias[:], 0.0).then_inc(const_ready, 1)
            by_expert = experts[:].rearrange("p (e m) -> p e m", e=E)[:, :, 2 * W:PART]
            g.memset(by_expert, 0.0).then_inc(made, 1)
            pool.wait_ge(made, 5)
            g.affine_select(out=by_expert, in_=by_expert, compare_op=ALU.not_equal, fill=1.0, base=0,
                            pattern=[[-1, E], [0, P]], channel_multiplier=1).then_inc(made, 1)
            pool.wait_ge(made, 6)
            g.affine_select(out=by_expert, in_=by_expert, compare_op=ALU.not_equal, fill=1.0, base=-LO,
                            pattern=[[-1, E], [0, P]], channel_multiplier=1).then_inc(const_ready, 1)

            def split_experts(pair):
                for k in range(2):
                    pool.wait_ge(ew_loaded[k], pair * 32 + 32)
                    g.tensor_tensor(wf[:, k, :], wf[:, k, :], wscale[:].broadcast_to([P, W]), ALU.mult).then_inc(ws_ready, 1)
                for k in range(2):
                    e = 2 * pair + k
                    pool.wait_ge(wh_ready, e + 1)
                    g.tensor_tensor(chunks(e, 1), wf_chunks(k), chunks(e, 0), ALU.subtract).then_inc(wl_ready, 1)

            def dispatch(gr, t0, t1):
                n = GROUPS[gr] * TB
                for t in range(t0, t1):
                    for k in range(TOPK):
                        c = k * n + t
                        g.indirect_dma_start(slots, bass.IndirectOffsetOnAxis(ap=slot_of[:, gr, c:c + 1], axis=0),
                                             rows[:, k, group_b0[gr] * TB + t, :], None).then_inc(dispatched[gr], 16)

            with pool.Fori(0, E // 2) as p:
                split_experts(p)
            pool.wait_ge(dispatch_ready, 1)
            pool.wait_ge(prefilled, 16 * -(-group_tiles[0] // PREFILL))
            pool.wait_ge(rows_copied[0], 16 * GROUPS[0])
            dispatch(0, 0, GROUPS[0] * TB)
            def give_back(j0, j1, gr):
                for j in range(j0, j1):
                    pool.wait_ge(y_ready, j + 1)
                    g.indirect_dma_start(returned, bass.IndirectOffsetOnAxis(ap=slot_meta[:, j, 1:2].bitcast(U32), axis=0),
                                         y[:, j, 0:D], None).then_inc(y_returned[gr], 16)

            pool.wait_ge(x1_kept, 16 * B)
            for b in range(B):
                x1_b = x1[:, b * TB:(b + 1) * TB, :]
                ins = g.tensor_tensor(x1_b, x1_b, lnb[:].rearrange("p (a d) -> p a d", a=1).broadcast_to([P, TB, D]), ALU.add)
            ins.then_inc(x1_ready, 1)
            EARLY = 2
            give_back(0, EARLY, 0)
            pool.wait_ge(dispatch_ready, 2)
            pool.wait_ge(prefilled, 16 * B)
            pool.wait_ge(rows_copied[1], 16 * GROUPS[1])
            dispatch(1, 0, GROUPS[1] * TB)
            give_back(EARLY, group_first[1], 0)
            sums_at = SUM_FROM * UNROLL - 1
            give_back(group_first[1], sums_at, 1)
            for u in range(TA // 2):
                give_back(sums_at + u, sums_at + u + 1, 1)
                for n in range(2):
                    if 2 * u == SETS[n][0]:
                        pool.wait_ge(pair_loaded[n], 16 * TOPK)
                two = slice(2 * u, 2 * u + 2)
                g.tensor_tensor(pair[0][:, two, :], pair[0][:, two, :], pair[1][:, two, :], ALU.add).then_inc(pairs_added, 1)
            give_back(sums_at + TA // 2, J, 1)

            for n, i in enumerate((1, 2)):
                t0, t1, _ = SETS[i]
                z_ = pair[0][:, t0:t1, :]
                pool.wait_ge(normed[i], 1)
                g.tensor_tensor(z_, z_, lng[:].rearrange("p (a d) -> p a d", a=1).broadcast_to([P, t1 - t0, D]),
                                ALU.mult).then_inc(scaled, 1)
                pool.wait_ge(scaled, n + 1)
                g.tensor_tensor(z_, z_, x1[:, t0:t1, :], ALU.add).then_inc(summed[i], 1)
                if n == 0:
                    t0, t1, _ = SETS[3]
                    pool.wait_ge(pair_loaded[3], 16 * TOPK)
                    g.tensor_tensor(pair[0][:, t0:t1, :], pair[0][:, t0:t1, :], pair[1][:, t0:t1, :], ALU.add).then_inc(added, 1)


_INS = ["L0_attn_embeddings", "L0_attn_W_Q", "L0_attn_W_K", "L0_attn_W_V", "L0_ffn_gate_w", "L0_ffn_gate_b",
        "L0_ffn_w1", "L0_ffn_b1", "L0_ffn_w2", "L0_ffn_b2", "L0_ffn_ln_g", "L0_ffn_ln_b"]


def kernel(**inputs):
    import numpy as _np
    import concourse.bacc as _bacc
    from concourse import mybir as _mybir
    from concourse.bass_utils import run_bass_kernel_spmd as _run

    nc = _bacc.Bacc("TRN2", target_bir_lowering=False, num_devices=1)
    arrays, args = {}, []
    for name in _INS:
        a = _np.ascontiguousarray(inputs[name])
        arrays[f"in_{name}_dram"] = a
        args.append(nc.dram_tensor(f"in_{name}_dram", a.shape, _mybir.dt.from_np(a.dtype), kind="ExternalInput").ap())
    shape = arrays["in_L0_attn_embeddings_dram"].shape
    args.append(nc.dram_tensor("out_0_dram", shape, _mybir.dt.float32, kind="ExternalOutput").ap())
    moe_block(nc, *args)
    r = _run(nc, [arrays], core_ids=[0])
    return r.results[0]["out_0_dram"]
```
